# Optimizing a Trainium2 kernel written in Bass

```python
import numpy as np
import jax
import jax.numpy as jnp

def _softmax(x, axis=-1):
    return jax.nn.softmax(x, axis=axis)
def _gelu(x):
    return jax.nn.gelu(x, approximate=True)
def _silu(x):
    return jax.nn.silu(x)
def _sigmoid(x):
    return jax.nn.sigmoid(x)
def _layernorm(x, axis=-1, eps=1e-5):
    m = jnp.mean(x, axis=axis, keepdims=True)
    v = jnp.var(x, axis=axis, keepdims=True)
    return (x - m) / jnp.sqrt(v + eps)
def _scatter_add(tgt, idx, src, axis=0):
    return tgt.at[idx].add(src)
def _segment_sum(src, seg, n):
    return jax.ops.segment_sum(src, seg, n)

kernel_name = 'mk_conv_seq_d1_conv_nchw256_22ac59'

def setup_inputs(seed: int = 0):
    np.random.seed(seed)
    _w = jnp.asarray
    def _rec_inputs():
        import jax
        import jax.numpy as jnp
        _gk = jax.random.key(seed)
        x = -0.0002023 + 1 * jax.random.normal(jax.random.fold_in(_gk, 1), (8, 256, 56, 56), jnp.float32)
        return x
    x = _rec_inputs()
    def _L0_conv_setup():
        import jax, jax.numpy as jnp
        import numpy as np
        DIM = 256
        NH = 4
        HD = DIM // 2
        HALF = DIM // 2
        DI = NH * HD
        B, H, W = (8, 56, 56)

        def _conv1x1(w, b, x):
            return jnp.einsum('oc,bchw->bohw', w, x) + b[None, :, None, None]

        def _mha(x, qw, qb, kw, kb, vw, vb, pw, pb, rel):
            Bx, C, Hx, Wx = x.shape
            q = _conv1x1(qw, qb, x).transpose(0, 2, 1, 3).reshape(Bx, Hx, NH, HD, Wx)
            k = _conv1x1(kw, kb, x).transpose(0, 2, 1, 3).reshape(Bx, Hx, NH, HD, Wx)
            v = _conv1x1(vw, vb, x).transpose(0, 2, 1, 3).reshape(Bx, Hx, NH, HD, Wx)
            att = jnp.einsum('bhndi,bhndj->bhnij', q, k) * HD ** (-0.5)
            L = Wx
            idx = (jnp.arange(L)[:, None] - jnp.arange(L)[None, :] + L - 1).reshape(-1)
            bias = jax.lax.stop_gradient(rel[:, idx].reshape(NH, L, L))
            att = jax.nn.softmax(att + bias[None, None], axis=-1)
            out = jnp.einsum('bhnij,bhndj->bhnid', att, v)
            out = out.reshape(Bx, Hx, Wx, NH * HD).transpose(0, 3, 1, 2)
            return _conv1x1(pw, pb, out) + x

        def _forward(x, xq_w, xq_b, xk_w, xk_b, xv_w, xv_b, xp_w, xp_b, rel_x, yq_w, yq_b, yk_w, yk_b, yv_w, yv_b, yp_w, yp_b, rel_y, cp_w, cp_b, m1_w, m1_b, m2_w, m2_b, ls1, ls2):
            ax, ay = jnp.split(x, 2, axis=1)
            ax = _mha(ax, xq_w, xq_b, xk_w, xk_b, xv_w, xv_b, xp_w, xp_b, rel_x)
            ay = _mha(ay.transpose(0, 1, 3, 2), yq_w, yq_b, yk_w, yk_b, yv_w, yv_b, yp_w, yp_b, rel_y).transpose(0, 1, 3, 2)
            net = _conv1x1(cp_w, cp_b, jnp.concatenate([ax, ay], axis=1))
            net = net * ls1[None] + x
            h = jax.nn.gelu(_conv1x1(m1_w, m1_b, net), approximate=False)
            out = _conv1x1(m2_w, m2_b, h)
            return out * ls2[None] + net
        key = jax.random.key(seed)
        ks = iter(jax.random.split(key, 32))

        def w(shape, s=0.05):
            return jax.random.normal(next(ks), shape, dtype=jnp.float32) * s
        return dict(x=jax.random.normal(next(ks), (B, DIM, H, W), dtype=jnp.float32), xq_w=w((DI, HALF)), xq_b=w((DI,)), xk_w=w((DI, HALF)), xk_b=w((DI,)), xv_w=w((DI, HALF)), xv_b=w((DI,)), xp_w=w((HALF, DI)), xp_b=w((HALF,)), rel_x=jax.random.normal(next(ks), (NH, W * W), dtype=jnp.float32), yq_w=w((DI, HALF)), yq_b=w((DI,)), yk_w=w((DI, HALF)), yk_b=w((DI,)), yv_w=w((DI, HALF)), yv_b=w((DI,)), yp_w=w((HALF, DI)), yp_b=w((HALF,)), rel_y=jax.random.normal(next(ks), (NH, H * H), dtype=jnp.float32), cp_w=w((DIM, DIM)), cp_b=w((DIM,)), m1_w=w((2 * DIM, DIM)), m1_b=w((2 * DIM,)), m2_w=w((DIM, 2 * DIM)), m2_b=w((DIM,)), ls1=jnp.ones((DIM, 1, 1), jnp.float32), ls2=jnp.ones((DIM, 1, 1), jnp.float32))
    _L0_conv_all = _L0_conv_setup()
    _L0_conv_in = {k: v for k, v in _L0_conv_all.items() if k in ('xq_w', 'xq_b', 'xk_w', 'xk_b', 'xv_w', 'xv_b', 'xp_w', 'xp_b', 'rel_x', 'yq_w', 'yq_b', 'yk_w', 'yk_b', 'yv_w', 'yv_b', 'yp_w', 'yp_b', 'rel_y', 'cp_w', 'cp_b', 'm1_w', 'm1_b', 'm2_w', 'm2_b', 'ls1', 'ls2', )}
    del _L0_conv_all

    return {
        "x": x,
        "L0_conv_xq_w": _L0_conv_in["xq_w"],
        "L0_conv_xq_b": _L0_conv_in["xq_b"],
        "L0_conv_xk_w": _L0_conv_in["xk_w"],
        "L0_conv_xk_b": _L0_conv_in["xk_b"],
        "L0_conv_xv_w": _L0_conv_in["xv_w"],
        "L0_conv_xv_b": _L0_conv_in["xv_b"],
        "L0_conv_xp_w": _L0_conv_in["xp_w"],
        "L0_conv_xp_b": _L0_conv_in["xp_b"],
        "L0_conv_rel_x": _L0_conv_in["rel_x"],
        "L0_conv_yq_w": _L0_conv_in["yq_w"],
        "L0_conv_yq_b": _L0_conv_in["yq_b"],
        "L0_conv_yk_w": _L0_conv_in["yk_w"],
        "L0_conv_yk_b": _L0_conv_in["yk_b"],
        "L0_conv_yv_w": _L0_conv_in["yv_w"],
        "L0_conv_yv_b": _L0_conv_in["yv_b"],
        "L0_conv_yp_w": _L0_conv_in["yp_w"],
        "L0_conv_yp_b": _L0_conv_in["yp_b"],
        "L0_conv_rel_y": _L0_conv_in["rel_y"],
        "L0_conv_cp_w": _L0_conv_in["cp_w"],
        "L0_conv_cp_b": _L0_conv_in["cp_b"],
        "L0_conv_m1_w": _L0_conv_in["m1_w"],
        "L0_conv_m1_b": _L0_conv_in["m1_b"],
        "L0_conv_m2_w": _L0_conv_in["m2_w"],
        "L0_conv_m2_b": _L0_conv_in["m2_b"],
        "L0_conv_ls1": _L0_conv_in["ls1"],
        "L0_conv_ls2": _L0_conv_in["ls2"],
    }

def reference(x, L0_conv_xq_w, L0_conv_xq_b, L0_conv_xk_w, L0_conv_xk_b, L0_conv_xv_w, L0_conv_xv_b, L0_conv_xp_w, L0_conv_xp_b, L0_conv_rel_x, L0_conv_yq_w, L0_conv_yq_b, L0_conv_yk_w, L0_conv_yk_b, L0_conv_yv_w, L0_conv_yv_b, L0_conv_yp_w, L0_conv_yp_b, L0_conv_rel_y, L0_conv_cp_w, L0_conv_cp_b, L0_conv_m1_w, L0_conv_m1_b, L0_conv_m2_w, L0_conv_m2_b, L0_conv_ls1, L0_conv_ls2):
    import jax
    import jax.numpy as jnp
    def _L0_conv_ref(x, xq_w, xq_b, xk_w, xk_b, xv_w, xv_b, xp_w, xp_b, rel_x, yq_w, yq_b, yk_w, yk_b, yv_w, yv_b, yp_w, yp_b, rel_y, cp_w, cp_b, m1_w, m1_b, m2_w, m2_b, ls1, ls2):
        import jax, jax.numpy as jnp
        import numpy as np
        DIM = 256
        NH = 4
        HD = DIM // 2
        HALF = DIM // 2
        DI = NH * HD
        B, H, W = (8, 56, 56)

        def _conv1x1(w, b, x):
            return jnp.einsum('oc,bchw->bohw', w, x) + b[None, :, None, None]

        def _mha(x, qw, qb, kw, kb, vw, vb, pw, pb, rel):
            Bx, C, Hx, Wx = x.shape
            q = _conv1x1(qw, qb, x).transpose(0, 2, 1, 3).reshape(Bx, Hx, NH, HD, Wx)
            k = _conv1x1(kw, kb, x).transpose(0, 2, 1, 3).reshape(Bx, Hx, NH, HD, Wx)
            v = _conv1x1(vw, vb, x).transpose(0, 2, 1, 3).reshape(Bx, Hx, NH, HD, Wx)
            att = jnp.einsum('bhndi,bhndj->bhnij', q, k) * HD ** (-0.5)
            L = Wx
            idx = (jnp.arange(L)[:, None] - jnp.arange(L)[None, :] + L - 1).reshape(-1)
            bias = jax.lax.stop_gradient(rel[:, idx].reshape(NH, L, L))
            att = jax.nn.softmax(att + bias[None, None], axis=-1)
            out = jnp.einsum('bhnij,bhndj->bhnid', att, v)
            out = out.reshape(Bx, Hx, Wx, NH * HD).transpose(0, 3, 1, 2)
            return _conv1x1(pw, pb, out) + x

        def _forward(x, xq_w, xq_b, xk_w, xk_b, xv_w, xv_b, xp_w, xp_b, rel_x, yq_w, yq_b, yk_w, yk_b, yv_w, yv_b, yp_w, yp_b, rel_y, cp_w, cp_b, m1_w, m1_b, m2_w, m2_b, ls1, ls2):
            ax, ay = jnp.split(x, 2, axis=1)
            ax = _mha(ax, xq_w, xq_b, xk_w, xk_b, xv_w, xv_b, xp_w, xp_b, rel_x)
            ay = _mha(ay.transpose(0, 1, 3, 2), yq_w, yq_b, yk_w, yk_b, yv_w, yv_b, yp_w, yp_b, rel_y).transpose(0, 1, 3, 2)
            net = _conv1x1(cp_w, cp_b, jnp.concatenate([ax, ay], axis=1))
            net = net * ls1[None] + x
            h = jax.nn.gelu(_conv1x1(m1_w, m1_b, net), approximate=False)
            out = _conv1x1(m2_w, m2_b, h)
            return out * ls2[None] + net
        return _forward(x, xq_w, xq_b, xk_w, xk_b, xv_w, xv_b, xp_w, xp_b, rel_x, yq_w, yq_b, yk_w, yk_b, yv_w, yv_b, yp_w, yp_b, rel_y, cp_w, cp_b, m1_w, m1_b, m2_w, m2_b, ls1, ls2)

    def _gn(v, G=32, eps=1e-5):
        B_, C_, H_, W_ = v.shape
        g = v.reshape(B_, G, C_ // G, H_, W_)
        m = jnp.mean(g, axis=(2, 3, 4), keepdims=True)
        s = jnp.var(g, axis=(2, 3, 4), keepdims=True)
        return ((g - m) / jnp.sqrt(s + eps)).reshape(v.shape)

    def _ln_c(v, eps=1e-6):
        m = jnp.mean(v, axis=1, keepdims=True)
        s = jnp.var(v, axis=1, keepdims=True)
        return (v - m) / jnp.sqrt(s + eps)

    def _ln_t(v, eps=1e-5):
        m = jnp.mean(v, axis=-1, keepdims=True)
        s = jnp.var(v, axis=-1, keepdims=True)
        return (v - m) / jnp.sqrt(s + eps)

    def _to_tokens(v):
        B_, C_, H_, W_ = v.shape
        return v.reshape(B_, C_, H_ * W_).transpose(0, 2, 1)
    def _from_tokens(t, like):
        B_, C_, H_, W_ = like.shape
        return t.transpose(0, 2, 1).reshape(B_, C_, H_, W_)

    x = _L0_conv_ref(x, L0_conv_xq_w, L0_conv_xq_b, L0_conv_xk_w, L0_conv_xk_b, L0_conv_xv_w, L0_conv_xv_b, L0_conv_xp_w, L0_conv_xp_b, L0_conv_rel_x, L0_conv_yq_w, L0_conv_yq_b, L0_conv_yk_w, L0_conv_yk_b, L0_conv_yv_w, L0_conv_yv_b, L0_conv_yp_w, L0_conv_yp_b, L0_conv_rel_y, L0_conv_cp_w, L0_conv_cp_b, L0_conv_m1_w, L0_conv_m1_b, L0_conv_m2_w, L0_conv_m2_b, L0_conv_ls1, L0_conv_ls2)
    return x


_drawn_inputs = setup_inputs


def setup_inputs(seed=0):
    import zlib

    import numpy as np

    out = dict(_drawn_inputs(seed))
    spreads = {'L0_conv_ls1': (1.0, 0.2), 'L0_conv_ls2': (1.0, 0.2)}
    factors = {'L0_conv_xq_w': 2.807,
     'L0_conv_xq_b': 8.0,
     'L0_conv_xk_w': 2.771,
     'L0_conv_xk_b': 8.0,
     'L0_conv_xp_b': 2.672,
     'L0_conv_yq_w': 2.804,
     'L0_conv_yq_b': 8.0,
     'L0_conv_yk_w': 2.804,
     'L0_conv_yk_b': 8.0,
     'L0_conv_yp_b': 2.716}
    for name, (base, spread) in spreads.items():
        noise = np.random.default_rng([zlib.crc32(name.encode()), seed]).standard_normal(out[name].shape)
        drawn = base * np.exp(spread * noise) if base else spread * noise
        out[name] = jnp.asarray(drawn.astype(out[name].dtype))
    for name, factor in factors.items():
        out[name] = (out[name] * factor).astype(out[name].dtype)
    return out
```

```python
from contextlib import ExitStack

import concourse.bass as bass
from concourse import mybir

F32 = mybir.dt.float32
F32R = mybir.dt.float32r
ALU = mybir.AluOpType
ACT = mybir.ActivationFunctionType
AX_X = mybir.AxisListType.X

P = 128
B, DIM, L = 8, 256, 56
HW = L * L
NH = 4
HALF = DIM // 2
HD = DIM // 2
SCALE = float(HD) ** -0.5
T = DIM // P
FT = 2 * DIM // P
SEQ = 4
BLK = 2 * SEQ * L
STEPS_IMG = L // (2 * SEQ)
STEPS = B * STEPS_IMG
LQ = L // NH
PAD = 64
QW = 2 * SEQ * L
NCOL = 30
C_QB, C_VB, C_PB, C_CPB, C_M1B, C_M2B, C_LS1, C_LS2 = 0, 8, 16, 18, 20, 24, 26, 28


def axial_block_kernel(nc, x, wq, wk, wv, wpT, cpT, m1T, m2T, columns, ls_rows, rel_tiled, out):
    ctx = ExitStack()
    with ctx:
        def sb(name, shape, dt=F32):
            return ctx.enter_context(nc.sbuf_tensor(name, shape, dt))

        def bank(name):
            return ctx.enter_context(nc.psum_tensor(name, [P, 512], F32))

        def sem(name):
            return ctx.enter_context(nc.semaphore(name))

        ident = sb("ident", [P, P])
        cols = sb("cols", [P, NCOL])
        ls_bc = sb("ls_bc", [P, 2, DIM])
        rel = sb("rel", [P, T, 2, 2, L])
        u_hi = sb("u_hi", [P, T, NH, P], F32R)
        u_lo = sb("u_lo", [P, T, NH, P], F32R)
        u_bias = sb("u_bias", [P, T, NH])
        o_w = sb("o_w", [P, T, NH, NH, P])
        o_bias = sb("o_bias", [P, T, NH])
        cp_w = sb("cp_w", [P, T, DIM])
        m1_hi = sb("m1_hi", [P, T, 2 * DIM], F32R)
        m1_lo = sb("m1_lo", [P, T, 2 * DIM], F32R)
        m2_w = sb("m2_w", [P, FT, DIM])
        m2_hi = sb("m2_hi", [P, FT, DIM], F32R)
        m2_lo = sb("m2_lo", [P, FT, DIM], F32R)
        cp_bias = sb("cp_bias", [P, T])
        m2_bias = sb("m2_bias", [P, T])
        y_image = sb("y_image", [P, 2 * HW])
        x_raw = sb("x_raw", [P, BLK])
        x_hi = sb("x_hi", [P, T, BLK], F32R)
        x_lo = sb("x_lo", [P, T, BLK], F32R)
        x_pad = sb("x_pad", [P, T, 2 * SEQ, PAD])
        u = sb("u", [P, T, 2 * SEQ, NH, PAD])
        x_t = sb("x_t", [P, 2, 2, P])
        score = sb("score", [P, QW])
        expd = sb("expd", [P, QW])
        row_max = sb("row_max", [P, 8])
        row_sum = sb("row_sum", [P, 8])
        row_rec = sb("row_rec", [P, 8])
        prob = sb("prob", [P, 8, PAD])
        prob_t = sb("prob_t", [P, 2, NH * L])
        z = sb("z", [P, NH, NH, 2 * SEQ, LQ])
        ax = sb("ax", [P, HW])
        ay = sb("ay", [P, 2 * HW])
        x_tail = sb("x_tail", [P, T, BLK])
        cp_in = sb("cp_in", [P, T, BLK])
        net = sb("net", [P, T, BLK])
        net_hi = sb("net_hi", [P, T, BLK], F32R)
        net_lo = sb("net_lo", [P, T, BLK], F32R)
        hid = sb("hid", [P, FT, BLK])
        hid_hi = sb("hid_hi", [P, FT, BLK], F32R)
        hid_lo = sb("hid_lo", [P, FT, BLK], F32R)

        stage = ay[:, 0:2 * 4 * NH * P].rearrange("p (b w h c) -> p b w h c", b=2, w=4, h=NH) \
            if 2 * HW >= 2 * 4 * NH * P else None
        st_q, st_k, st_v, st_p = (stage[:, :, w] for w in range(4))
        st_cp = ax[:, 0:T * DIM].rearrange("p (t o) -> p t o", t=T)
        st_m1 = ax[:, T * DIM:3 * T * DIM].rearrange("p (t o) -> p t o", t=T)
        st_m2 = hid[:, :, 0:DIM]

        ps_score = bank("ps_score")
        ps_pt = bank("ps_pt")
        ps_z = [bank("ps_z0"), bank("ps_z1")]
        ps_un = [bank("ps_un0"), bank("ps_un1")]
        ps_mlp = [bank("ps_mlp0"), bank("ps_mlp1")]

        ps_o = [ps_un[1], ps_score, ps_pt, ps_z[0]]

        weights_in = sem("weights_in")
        rel_in = sem("rel_in")
        rel_zeroed = sem("rel_zeroed")
        pads_zeroed = sem("pads_zeroed")
        ident_made = sem("ident_made")
        prep_mm = sem("prep_mm")
        prep_act = sem("prep_act")
        prep_dve = sem("prep_dve")
        y_loaded = sem("y_loaded")
        x_loaded = sem("x_loaded")
        tail_loaded = sem("tail_loaded")
        stored = sem("stored")
        xhi_made = sem("xhi_made")
        xlo_made = sem("xlo_made")
        xpad_made = sem("xpad_made")
        xt_done = sem("xt_done")
        xt_out = sem("xt_out")
        pt_done = sem("pt_done")
        pt_out = sem("pt_out")
        s_done = sem("s_done")
        added = sem("added")
        maxed = sem("maxed")
        shifted = sem("shifted")
        exped = sem("exped")
        summed = sem("summed")
        inverted = sem("inverted")
        prob_made = sem("prob_made")
        z_done = sem("z_done")
        z0_out = sem("z0_out")
        z1_out = sem("z1_out")
        u_done = sem("u_done")
        u_out = sem("u_out")
        o_done = sem("o_done")
        o_out = sem("o_out")
        cpin_made = sem("cpin_made")
        cp_done = sem("cp_done")
        net_made = sem("net_made")
        nethi_made = sem("nethi_made")
        netlo_made = sem("netlo_made")
        m1_done = sem("m1_done")
        hid_made = sem("hid_made")
        hidhi_made = sem("hidhi_made")
        hidlo_made = sem("hidlo_made")
        m2_done = sem("m2_done")
        out_made = sem("out_made")

        x_v = x
        out_v = out

        def chunk_of(ap, c, t0, nt):
            src = ap[bass.ds(c // STEPS_IMG, 1), t0 * P:(t0 + nt) * P, bass.ds((c % STEPS_IMG) * BLK, BLK)]
            return src.rearrange("b (t p) n -> p (b t) n", p=P)

        def y_block(buf, s):
            v = buf[:, :].rearrange("p (a h w) -> p a w h", a=2, h=L)
            img, q = s // STEPS_IMG, s % STEPS_IMG
            return v[:, bass.ds(img % 2, 1), bass.ds(q * 2 * SEQ, 2 * SEQ), :].rearrange("p a w h -> p (a w) h")

        block = ctx.enter_context(nc.Block())

        @block.sync
        def _(sp):
            for b in range(T):
                for w, src in enumerate((wq, wk, wv, wpT)):
                    sp.dma_start(stage[:, b, w], src[b].rearrange("(h d) c -> d h c", d=P)).then_inc(weights_in, 16)
            sp.dma_start(st_cp, cpT.rearrange("(t p) o -> p t o", p=P)).then_inc(weights_in, 16)
            sp.dma_start(st_m1, m1T.rearrange("(t p) o -> p t o", p=P)).then_inc(weights_in, 16)
            sp.dma_start(st_m2, m2T.rearrange("(t p) o -> p t o", p=P)).then_inc(weights_in, 16)
            for q in range(STEPS_IMG):
                sp.dma_start(y_image[:, q * BLK:(q + 1) * BLK], chunk_of(x_v, q, 1, 1)[:, 0, :]).then_inc(y_loaded, 16)
            sp.dma_start(x_raw[:, :], chunk_of(x_v, 0, 0, 1)[:, 0, :]).then_inc(x_loaded, 16)

            def load_y(s):
                sp.wait_ge(xpad_made, 2 * s + 2)
                sp.wait_ge(xlo_made, 2 * s + 2)
                n = s + STEPS_IMG
                at = (n // STEPS_IMG) % 2 * HW + n % STEPS_IMG * BLK
                sp.dma_start(y_image[:, bass.ds(at, BLK)], chunk_of(x_v, n, 1, 1)[:, 0, :]).then_inc(y_loaded, 16)

            def load_x(s):
                sp.wait_ge(xpad_made, 2 * s - 1)
                sp.wait_ge(xlo_made, 2 * s - 1)
                sp.dma_start(x_raw[:, :], chunk_of(x_v, s, 0, 1)[:, 0, :]).then_inc(x_loaded, 16)

            def load_tail(c):
                sp.dma_start(x_tail[:, :, :], chunk_of(x_v, c, 0, T)).then_inc(tail_loaded, 16)

            def step(s, y=False, xr=False, tail=False, more=False):
                c = s - STEPS_IMG
                if y:
                    load_y(s)
                if more:
                    sp.wait_ge(net_made, 2 * c + 2)
                    load_tail(c + 1)
                if xr:
                    load_x(s + 2)
                if tail:
                    sp.wait_ge(out_made, 2 * c + 4)
                    sp.dma_start(chunk_of(out_v, c, 0, T), net[:, :, :]).then_inc(stored, 16)

            load_x(1)
            with sp.Fori(0, STEPS_IMG) as s:
                step(s, y=True, xr=True)
            load_tail(0)
            with sp.Fori(STEPS_IMG, STEPS - STEPS_IMG) as s:
                step(s, y=True, xr=True, tail=True, more=True)
            with sp.Fori(STEPS - STEPS_IMG, STEPS - 2) as s:
                step(s, xr=True, tail=True, more=True)
            with sp.Fori(STEPS - 2, STEPS + STEPS_IMG - 1) as s:
                step(s, tail=True, more=True)
            step(STEPS + STEPS_IMG - 1, tail=True)
            sp.wait_ge(stored, 16 * (STEPS + 1))

        @block.tensor
        def _(pe):
            mm = nc.tensor.matmul

            pe.wait_ge(weights_in, 16 * 11)
            pe.wait_ge(rel_in, 16 * (1 + 2 * T * NH + 2))
            for b in range(T):
                if b == 1:
                    pe.wait_ge(prep_act, 1)
                    pe.wait_ge(prep_dve, 7)
                for h in range(NH):
                    mm(ps_un[0][:, h * P:(h + 1) * P], st_q[:, b, h], st_k[:, b, h], start=True, stop=True)
                    mm(ps_o[h][:, :], st_v[:, b, h], st_p[:, b].rearrange("p m o -> p (m o)"), start=True, stop=True)
                for h in range(NH):
                    mm(ps_mlp[0][:, h:h + 1], st_k[:, b, h], cols[:, C_QB + b * NH + h:C_QB + b * NH + h + 1],
                       start=True, stop=True)
                for m in range(NH):
                    last = mm(ps_mlp[1][:, 0:NH], st_p[:, b, m], cols[:, C_VB + b * NH:C_VB + (b + 1) * NH],
                              start=(m == 0), stop=(m == NH - 1))
                last.then_inc(prep_mm, 1)
            pe.sem_inc(s_done, 2)
            pe.sem_inc(z_done, 1)
            pe.sem_inc(o_done, 1)
            pe.sem_inc(cp_done, 2)
            pe.sem_inc(m1_done, 4)
            pe.sem_inc(m2_done, 2)
            pe.wait_ge(ident_made, 2)
            pe.wait_ge(pads_zeroed, 3)
            pe.wait_ge(prep_act, 2)
            pe.wait_ge(prep_dve, 19)

            def three(ps, w_hi, w_lo, a_hi, a_lo, first, last):
                mm(ps, w_lo, a_hi, start=first, stop=False)
                mm(ps, w_hi, a_lo, start=False, stop=False)
                return mm(ps, w_hi, a_hi, start=False, stop=last)

            def values_t(g, k):
                br, kk = k // 2, k % 2
                pe.wait_ge(xpad_made, g // 2 + 1 if isinstance(g, int) else 2 * ((g - k) // 4) + br + 1)
                if not isinstance(g, int) or g:
                    pe.wait_ge(z0_out, g)
                    pe.wait_ge(xt_out, g)
                for pair in range(2):
                    last = nc.tensor.transpose(ps_z[0][:, pair * P:(pair + 1) * P],
                                               x_pad[:, br, 4 * kk + 2 * pair:4 * kk + 2 * pair + 2, :]
                                               .rearrange("p s i -> p (s i)"), ident[:, :])
                last.then_inc(xt_done, 1)

            def scores(g, blk, k):
                br, kk = k // 2, k % 2
                pe.wait_ge(u_out, 4 * blk + 4)
                if not isinstance(g, int) or g:
                    pe.wait_ge(added, g)
                for pair in range(2):
                    for hp in range(2):
                        for sq in range(2):
                            n = 4 * kk + 2 * pair + sq
                            at = ((pair * 2 + hp) * 2 + sq) * L
                            last = mm(ps_score[:, at:at + L],
                                      u[:, br, n, 2 * hp:2 * hp + 2, :].rearrange("p h i -> p (h i)"),
                                      x_pad[:, br, n, 0:L], start=True, stop=True)
                last.then_inc(s_done, 1)

            def probs_t(g):
                pe.wait_ge(prob_made, g + 1)
                pe.wait_ge(pt_out, g + 1)
                for n in range(4):
                    last = nc.tensor.transpose(ps_pt[:, n * P:(n + 1) * P],
                                               prob[:, 2 * n:2 * n + 2, :].rearrange("p s j -> p (s j)"),
                                               ident[:, :])
                last.then_inc(pt_done, 1)

            def weigh(g, k, more):
                pe.wait_ge(pt_out, g + 2)
                pe.wait_ge(xt_out, g + 2 if more else g + 1)
                pe.wait_ge(z1_out, g + 1)
                pe.wait_ge(z0_out, g + 1)
                for pair in range(2):
                    for sq in range(2):
                        rows = slice(PAD * sq, PAD * sq + L)
                        last = mm(ps_z[sq][:, pair * NH * L:(pair + 1) * NH * L], x_t[rows, k % 2, pair, :],
                                  prob_t[rows, pair, :], start=True, stop=True)
                last.then_inc(z_done, 1)

            def queries(m, blk, h, bk, free):
                br = h[1]
                pe.wait_ge(xhi_made, blk + 1)
                pe.wait_ge(xlo_made, blk + 1)
                if free is not None:
                    pe.wait_ge(*free)
                three(ps_un[bk][:, 0:BLK], u_hi[:, br, h[0]], u_lo[:, br, h[0]], x_hi[:, br, :], x_lo[:, br, :],
                      True, True).then_inc(u_done, 1)

            def project(blk, br, g, bk, free):
                pe.wait_ge(z0_out, g + 2)
                pe.wait_ge(z1_out, g + 2)
                pe.wait_ge(*free)
                n = BLK // NH
                for h in range(NH):
                    for m in range(NH):
                        last = mm(ps_un[bk][:, h * n:(h + 1) * n], o_w[:, br, h, m],
                                  z[:, h, m].rearrange("p s i -> p (s i)"), start=(m == 0), stop=(m == NH - 1))
                last.then_inc(o_done, 1)

            def mlp(c, k):
                if k == 0:
                    for t in range(T):
                        pe.wait_ge(cpin_made, 2 * c + 2)
                        pe.wait_ge(out_made, 2 * c + 1 + t)
                        for i in range(T):
                            last = mm(ps_mlp[t][:, 0:BLK], cp_w[:, i, t * P:(t + 1) * P], cp_in[:, i, :],
                                      start=(i == 0), stop=(i == T - 1))
                        last.then_inc(cp_done, 1)
                if k == 2:
                    for t in range(FT):
                        pe.wait_ge(nethi_made, c + 1)
                        pe.wait_ge(netlo_made, c + 1)
                        if t < 2:
                            pe.wait_ge(net_made, 2 * c + 1 + t)
                        else:
                            pe.wait_ge(hid_made, 4 * c + t - 1)
                        for i in range(T):
                            last = three(ps_mlp[t % 2][:, 0:BLK], m1_hi[:, i, t * P:(t + 1) * P],
                                         m1_lo[:, i, t * P:(t + 1) * P], net_hi[:, i, :], net_lo[:, i, :],
                                         i == 0, i == T - 1)
                        last.then_inc(m1_done, 1)
                if k == 3:
                    for t in range(T):
                        pe.wait_ge(hidhi_made, c + 2)
                        pe.wait_ge(hidlo_made, 2 * c + 4)
                        pe.wait_ge(hid_made, 4 * c + 4)
                        for i in range(FT):
                            last = three(ps_mlp[t][:, 0:BLK], m2_hi[:, i, t * P:(t + 1) * P],
                                         m2_lo[:, i, t * P:(t + 1) * P], hid_hi[:, i, :], hid_lo[:, i, :],
                                         i == 0, i == FT - 1)
                        last.then_inc(m2_done, 1)

            jobs = [("u", 0), ("u", 1), ("u", 2), ("u", 3), ("o", 0), ("u", 4), ("u", 5), ("u", 6), ("u", 7), ("o", 1)]

            def freed(s, n, emitted):
                for j in range(n - 2, -1, -2):
                    kind, i = jobs[j]
                    if kind == "o":
                        return o_out, 2 * s + i + 3
                    if i in emitted:
                        return u_out, 8 * s + 6 + i + 1
                return (u_out, 8 * s + 6) if n == 0 or n == 1 and isinstance(s, int) and s == 0 else (o_out, 2 * s + 2)

            def step(s, tail, last=False):
                emitted = set()
                n = 0
                for k in range(4):
                    g = 4 * s + k
                    more = not (last and k == 3)
                    if more:
                        values_t(g + 1, (k + 1) % 4)
                    probs_t(g)
                    if more:
                        scores(g + 1, 2 * s + (k + 1) // 2, (k + 1) % 4)
                    weigh(g, k, more)
                    for hh in range(2):
                        if not (last and k > 0):
                            head = 2 * ((k + 3) % 2) + hh
                            blk = 2 * s + (k + 3) // 2
                            queries(None, blk, (head, (k + 3) // 2 % 2), n % 2, freed(s, n, emitted))
                            emitted.add(2 * k + hh)
                        n += 1
                    if tail:
                        mlp(s - STEPS_IMG, k)
                    if k % 2:
                        project(2 * s + k // 2, k // 2, g, n % 2, freed(s, n, emitted))
                        n += 1

            for m in range(6):
                queries(m, m // 4, (m % 4, m // 4), m % 2, (u_out, m - 1) if m >= 2 else None)
            values_t(0, 0)
            scores(0, 0, 0)
            with pe.Fori(0, STEPS_IMG) as s:
                step(s, False)
            with pe.Fori(STEPS_IMG, STEPS - 1) as s:
                step(s, True)
            step(STEPS - 1, True, last=True)
            with pe.Fori(STEPS, STEPS + STEPS_IMG) as s:
                for k in range(4):
                    mlp(s - STEPS_IMG, k)

        @block.scalar
        def _(act):
            act.dma_start(cols[:, :], columns).then_inc(rel_in, 16)
            for n in range(2):
                act.dma_start(ls_bc[:, n, :], ls_rows[n:n + 1, :].to_broadcast([P, DIM])).then_inc(rel_in, 16)
            act.wait_ge(rel_zeroed, 1)
            for b in range(T):
                for h in range(NH):
                    w = 2 * L - 1
                    src = rel_tiled[b, h, L - 1:L - 1 + L * (w - 1)].rearrange("(i j) -> i j", j=w - 1)[:, 0:L]
                    for sq in range(2):
                        act.dma_start(rel[PAD * (h % 2):PAD * (h % 2) + L, b, h // 2, sq, :], src).then_inc(rel_in, 16)
            for b in range(T):
                act.wait_ge(prep_mm, b + 1)
                nc.scalar.activation(u_hi[:, b].rearrange("p h c -> p (h c)"), ps_un[0][:, :], ACT.Copy,
                                     scale=SCALE).then_inc(prep_act, 1)
                if b == 0:
                    act.wait_ge(prep_dve, 1)
            act.sem_inc(pt_out, 1)
            act.sem_inc(z1_out, 1)

            def query_out(m, blk, h, br):
                act.wait_ge(u_done, m + 1)
                if not isinstance(m, int) or blk:
                    act.wait_ge(s_done, 2 * blk)
                nc.scalar.activation(u[:, br, :, h, 0:L], ps_un[m % 2 if isinstance(m, int) else bank_of[0]][:, 0:BLK]
                                     .rearrange("p (s i) -> p s i", i=L), ACT.Identity,
                                     bias=u_bias[:, br, h:h + 1]).then_inc(u_out, 1)

            bank_of = [0]

            def exps(g):
                act.wait_ge(shifted, g + 1)
                if not isinstance(g, int) or g:
                    act.wait_ge(prob_made, g)
                nc.scalar.activation(expd[:, :], score[:, :], ACT.Exp).then_inc(exped, 1)

            def step(s, tail, last=False):
                n = 0
                c = s - STEPS_IMG
                for k in range(4):
                    g = 4 * s + k
                    act.wait_ge(pt_done, g + 1)
                    act.wait_ge(z_done, g + 1)
                    nc.scalar.activation(prob_t[:, :, :].rearrange("p a (h m i) -> p (a h) m i", m=NH, i=LQ),
                                         ps_pt[:, :].rearrange("p (n i m) -> p n m i", i=PAD // NH, m=NH)[:, :, :, 0:LQ],
                                         ACT.Copy).then_inc(pt_out, 1)
                    if not (last and k == 3):
                        exps(g + 1)
                    act.wait_ge(z_done, g + 2)
                    if k % 2 == 0:
                        act.wait_ge(o_done, 2 * s + k // 2 + 1)
                    take_z(nc.scalar, 1, k).then_inc(z1_out, 1)
                    for hh in range(2):
                        if not (last and k > 0):
                            bank_of[0] = n % 2
                            query_out(8 * s + 2 * k + 6 + hh, 2 * s + (k + 3) // 2, 2 * ((k + 3) % 2) + hh,
                                      (k + 3) // 2 % 2)
                        n += 1
                    n += k % 2
                    if tail:
                        mlp(c, k)

            def take_z(eng, sq, k):
                src = ps_z[sq][:, 0:2 * NH * L].rearrange("p (a n i) -> p a n i", a=2, i=LQ)
                dst = z[:, :, :, :, :].rearrange("p h m (q a s) i -> p q s a (h m) i", q=2, a=2)[:, k % 2, sq]
                return eng.activation(dst, src, ACT.Copy)

            def mlp(c, k):
                if k == 0:
                    act.wait_ge(net_made, 2 * c + 2)
                    act.wait_ge(m1_done, 4 * c + 4)
                    nc.scalar.activation(net_hi[:, :, :].rearrange("p t n -> p (t n)"),
                                         net[:, :, :].rearrange("p t n -> p (t n)"), ACT.Copy).then_inc(nethi_made, 1)
                if k == 2:
                    act.wait_ge(hidhi_made, c + 1)
                    act.wait_ge(hidlo_made, 2 * c + 2)
                    for t in range(FT):
                        act.wait_ge(m1_done, 4 * c + t + 5)
                        nc.scalar.activation(hid[:, t, :], ps_mlp[t % 2][:, 0:BLK], ACT.Gelu,
                                             bias=cols[:, C_M1B + t:C_M1B + t + 1]).then_inc(hid_made, 1)

            act.wait_ge(prep_dve, 19)
            act.wait_ge(pads_zeroed, 3)
            for m in range(6):
                query_out(m, m // 4, m % 4, m // 4)
            exps(0)
            with act.Fori(0, STEPS_IMG) as s:
                step(s, False)
            with act.Fori(STEPS_IMG, STEPS - 1) as s:
                step(s, True)
            step(STEPS - 1, True, last=True)
            with act.Fori(STEPS, STEPS + STEPS_IMG) as s:
                for k in range(4):
                    mlp(s - STEPS_IMG, k)

        @block.vector
        def _(dve):
            nc.vector.memset(rel[:, :, :, :, :], 0.0).then_inc(rel_zeroed, 1)
            nc.vector.memset(x_pad[:, :, :, :], 0.0).then_inc(pads_zeroed, 1)
            nc.vector.memset(u[:, :, :, :, :], 0.0).then_inc(pads_zeroed, 1)
            nc.vector.memset(prob[:, :, :], 0.0).then_inc(pads_zeroed, 1)
            dve.wait_ge(weights_in, 16 * 11)
            dve.wait_ge(rel_in, 16 * (1 + 2 * T * NH + 2))
            dve.wait_ge(prep_mm, 1)
            for b in range(T):
                if b:
                    dve.wait_ge(prep_mm, 2)
                dve.wait_ge(prep_act, b + 1)
                nc.vector.scalar_tensor_tensor(out=u_lo[:, b].rearrange("p h c -> p (h c)"), in0=ps_un[0][:, :],
                                               scalar=SCALE, in1=u_hi[:, b].rearrange("p h c -> p (h c)").bitcast(F32),
                                               op0=ALU.mult, op1=ALU.subtract).then_inc(prep_dve, 1)
                for h in range(NH):
                    nc.vector.tensor_copy(o_w[:, b, h].rearrange("p m o -> p (m o)"), ps_o[h][:, :]).then_inc(prep_dve, 1)
                nc.vector.tensor_scalar(u_bias[:, b, :], ps_mlp[0][:, 0:NH], SCALE, None, ALU.mult).then_inc(prep_dve, 1)
                nc.vector.tensor_scalar(o_bias[:, b, :], ps_mlp[1][:, 0:NH], cols[:, C_PB + b:C_PB + b + 1], None,
                                        ALU.add).then_inc(prep_dve, 1)
            for i in range(T):
                nc.vector.tensor_tensor(cp_w[:, i, :], st_cp[:, i, :], ls_bc[:, 0, :], ALU.mult)
            nc.vector.tensor_tensor(cp_bias[:, :], cols[:, C_CPB:C_CPB + T], cols[:, C_LS1:C_LS1 + T], ALU.mult)
            nc.vector.tensor_tensor(m2_bias[:, :], cols[:, C_M2B:C_M2B + T], cols[:, C_LS2:C_LS2 + T], ALU.mult)
            for i in range(FT):
                last = nc.vector.tensor_tensor(m2_w[:, i, :], st_m2[:, i, :], ls_bc[:, 1, :], ALU.mult)
            last.then_inc(prep_dve, 1)
            nc.vector.tensor_copy(m1_hi[:, :, :].rearrange("p t o -> p (t o)"),
                                  st_m1.rearrange("p t o -> p (t o)")).then_inc(prep_dve, 1)
            dve.wait_ge(prep_dve, 15)
            nc.vector.tensor_copy(m2_hi[:, :, :].rearrange("p t o -> p (t o)"),
                                  m2_w[:, :, :].rearrange("p t o -> p (t o)")).then_inc(prep_dve, 1)
            dve.wait_ge(prep_dve, 16)
            nc.vector.tensor_tensor(m1_lo[:, :, :].rearrange("p t o -> p (t o)"), st_m1.rearrange("p t o -> p (t o)"),
                                    m1_hi[:, :, :].rearrange("p t o -> p (t o)").bitcast(F32),
                                    ALU.subtract).then_inc(prep_dve, 1)
            dve.wait_ge(prep_dve, 17)
            nc.vector.tensor_tensor(m2_lo[:, :, :].rearrange("p t o -> p (t o)"),
                                    m2_w[:, :, :].rearrange("p t o -> p (t o)"),
                                    m2_hi[:, :, :].rearrange("p t o -> p (t o)").bitcast(F32),
                                    ALU.subtract).then_inc(prep_dve, 1)
            dve.wait_ge(prep_dve, 19)
            dve.wait_ge(pads_zeroed, 3)
            dve.sem_inc(z0_out, 1)
            dve.sem_inc(o_out, 2)
            dve.sem_inc(hidhi_made, 1)
            dve.sem_inc(hidlo_made, 2)
            dve.sem_inc(out_made, 2)
            dve.sem_inc(stored, 16)

            def split_hi(blk, s, br):
                if br == 0:
                    dve.wait_ge(x_loaded, 16 * s + 16)
                    src = x_raw[:, :].rearrange("p (s i) -> p s i", i=L)
                else:
                    dve.wait_ge(y_loaded, 16 * STEPS_IMG * (s // STEPS_IMG + 1))
                    src = y_block(y_image, s)
                if not isinstance(blk, int) or blk >= 2:
                    dve.wait_ge(u_done, 4 * blk - 4)
                nc.vector.tensor_scalar(x_hi[:, br, :].rearrange("p (s i) -> p s i", i=L), src, 1.0, None,
                                        ALU.mult).then_inc(xhi_made, 1)

            def pad(blk, s, br):
                src = x_raw[:, :].rearrange("p (s i) -> p s i", i=L) if br == 0 else y_block(y_image, s)
                if not isinstance(blk, int) or blk >= 2:
                    dve.wait_ge(s_done, 2 * blk)
                    dve.wait_ge(xt_done, 2 * blk - 2)
                nc.vector.tensor_scalar(x_pad[:, br, :, 0:L], src, 1.0, None, ALU.mult).then_inc(xpad_made, 1)

            def softmax_a(g, k):
                br = k // 2
                dve.wait_ge(s_done, g + 3)
                if not isinstance(g, int) or g:
                    dve.wait_ge(exped, g)
                nc.vector.tensor_tensor(score[:, :].rearrange("p (a n) -> p a n", a=2),
                                        ps_score[:, 0:QW].rearrange("p (a n) -> p a n", a=2),
                                        rel[:, br].rearrange("p h s j -> p (h s j)").unsqueeze(1)
                                        .to_broadcast([P, 2, QW // 2]), ALU.add).then_inc(added, 1)
                rows = score[:, :].rearrange("p (n j) -> p n j", j=L)
                dve.wait_ge(added, g + 1)
                nc.vector.tensor_reduce(row_max[:, :], rows, AX_X, ALU.max).then_inc(maxed, 1)
                dve.wait_ge(maxed, g + 1)
                nc.vector.tensor_tensor(rows, rows, row_max[:, :].unsqueeze(2).to_broadcast([P, 8, L]),
                                        ALU.subtract).then_inc(shifted, 1)

            def softmax_b(g):
                dve.wait_ge(exped, g + 1)
                nc.vector.tensor_reduce(row_sum[:, :], expd[:, :].rearrange("p (n j) -> p n j", j=L), AX_X,
                                        ALU.add).then_inc(summed, 1)
                dve.wait_ge(summed, g + 1)
                if not isinstance(g, int) or g:
                    dve.wait_ge(prob_made, g)
                nc.vector.reciprocal(row_rec[:, :], row_sum[:, :]).then_inc(inverted, 1)

            def values_out(g, k):
                dve.wait_ge(xt_done, g + 1)
                if not isinstance(g, int) or g:
                    dve.wait_ge(z_done, g)
                nc.vector.tensor_copy(x_t[:, k % 2].rearrange("p a c -> p (a c)"),
                                      ps_z[0][:, 0:2 * P]).then_inc(xt_out, 1)

            def step(s, tail, last=False):
                c = s - STEPS_IMG
                for k in range(4):
                    g = 4 * s + k
                    more = not (last and k == 3)
                    if more:
                        values_out(g + 1, (k + 1) % 4)
                        softmax_a(g + 1, (k + 1) % 4)
                    dve.wait_ge(z_done, g + 2)
                    if k % 2 == 0:
                        dve.wait_ge(o_done, 2 * s + k // 2 + 1)
                    src = ps_z[0][:, 0:2 * NH * L].rearrange("p (a n i) -> p a n i", a=2, i=LQ)
                    dst = z[:, :, :, :, :].rearrange("p h m (q a s) i -> p q s a (h m) i", q=2, a=2)[:, k % 2, 0]
                    nc.vector.tensor_copy(dst, src).then_inc(z0_out, 1)
                    if more:
                        softmax_b(g + 1)
                    if not last:
                        if k % 2 == 0:
                            split_hi(2 * s + 2 + k // 2, s + 1, k // 2)
                        else:
                            pad(2 * s + 2 + k // 2, s + 1, k // 2)
                    if tail:
                        mlp(c, k)
                    if k % 2:
                        dve.wait_ge(o_done, 2 * s + k // 2 + 2)
                        if tail:
                            dve.wait_ge(cpin_made, 2 * c + 2)
                        src = ps_un[(4 if k == 1 else 9) % 2][:, 0:BLK].rearrange("p (n s i) -> p n s i", n=NH, i=LQ)
                        if k == 1:
                            dst = ax[:, bass.ds(s % STEPS_IMG * BLK, BLK)].rearrange("p (s n i) -> p n s i", n=NH, i=LQ)
                        else:
                            dst = y_block(ay, s).rearrange("p s (n i) -> p n s i", n=NH)
                        bias = o_bias[:, k // 2, :].unsqueeze(2).unsqueeze(3).to_broadcast([P, NH, 2 * SEQ, LQ])
                        nc.vector.tensor_tensor(dst, src, bias, ALU.add).then_inc(o_out, 1)

            def mlp(c, k):
                if k == 0:
                    for t in range(T):
                        dve.wait_ge(cp_done, 2 * c + t + 3)
                        dve.wait_ge(stored, 16 * c + 16)
                        dve.wait_ge(tail_loaded, 16 * c + 16)
                        nc.vector.scalar_tensor_tensor(out=net[:, t, :], in0=ps_mlp[t][:, 0:BLK],
                                                       scalar=cp_bias[:, t:t + 1], in1=x_tail[:, t, :],
                                                       op0=ALU.add, op1=ALU.add).then_inc(net_made, 1)
                if k == 3:
                    dve.wait_ge(hid_made, 4 * c + 4)
                    dve.wait_ge(m2_done, 2 * c + 2)
                    nc.vector.tensor_copy(hid_hi[:, :, :].rearrange("p t n -> p (t n)"),
                                          hid[:, :, :].rearrange("p t n -> p (t n)")).then_inc(hidhi_made, 1)
                    dve.wait_ge(hidhi_made, c + 2)
                    nc.vector.tensor_tensor(hid_lo[:, 0:2, :].rearrange("p t n -> p (t n)"),
                                            hid[:, 0:2, :].rearrange("p t n -> p (t n)"),
                                            hid_hi[:, 0:2, :].rearrange("p t n -> p (t n)").bitcast(F32),
                                            ALU.subtract).then_inc(hidlo_made, 1)
                    for t in range(T):
                        dve.wait_ge(m2_done, 2 * c + t + 3)
                        nc.vector.scalar_tensor_tensor(out=net[:, t, :], in0=ps_mlp[t][:, 0:BLK],
                                                       scalar=m2_bias[:, t:t + 1], in1=net[:, t, :],
                                                       op0=ALU.add, op1=ALU.add).then_inc(out_made, 1)

            for b in range(T):
                split_hi(b, 0, b)
                pad(b, 0, b)
            values_out(0, 0)
            softmax_a(0, 0)
            softmax_b(0)
            with dve.Fori(0, STEPS_IMG) as s:
                step(s, False)
            with dve.Fori(STEPS_IMG, STEPS - 1) as s:
                step(s, True)
            step(STEPS - 1, True, last=True)
            with dve.Fori(STEPS, STEPS + STEPS_IMG) as s:
                for k in range(4):
                    mlp(s - STEPS_IMG, k)

        @block.gpsimd
        def _(pool):
            nc.gpsimd.memset(ident[:, :], 0.0).then_inc(ident_made, 1)
            pool.wait_ge(ident_made, 1)
            nc.gpsimd.affine_select(out=ident[:, :], in_=ident[:, :], compare_op=ALU.not_equal, fill=1.0, base=0,
                                    pattern=[[-1, P]], channel_multiplier=1).then_inc(ident_made, 1)

            pool.wait_ge(pads_zeroed, 3)

            def split_lo(blk, s, br):
                pool.wait_ge(xhi_made, blk + 1)
                pool.wait_ge(ident_made, 2)
                src = x_raw[:, :].rearrange("p (s i) -> p s i", i=L) if br == 0 else y_block(y_image, s)
                nc.gpsimd.tensor_tensor(x_lo[:, br, :].rearrange("p (s i) -> p s i", i=L), src,
                                        x_hi[:, br, :].rearrange("p (s i) -> p s i", i=L).bitcast(F32),
                                        ALU.subtract).then_inc(xlo_made, 1)

            def normalise(g):
                pool.wait_ge(inverted, g + 1)
                if not isinstance(g, int) or g:
                    pool.wait_ge(pt_done, g)
                nc.gpsimd.tensor_tensor(prob[:, :, 0:L], expd[:, :].rearrange("p (n j) -> p n j", j=L),
                                        row_rec[:, :].unsqueeze(2).to_broadcast([P, 8, L]),
                                        ALU.mult).then_inc(prob_made, 1)

            def mlp(c, k, s):
                if k == 0:
                    pool.wait_ge(tail_loaded, 16 * c + 16)
                    pool.wait_ge(o_out, 2 * s + 2 if s is not None else 2 * STEPS + 2)
                    pool.wait_ge(cp_done, 2 * c + 2)
                    pool.wait_ge(ident_made, 2)
                    at = c % STEPS_IMG * BLK
                    nc.gpsimd.tensor_tensor(cp_in[:, 0, :], ax[:, bass.ds(at, BLK)], x_tail[:, 0, :],
                                            ALU.add).then_inc(cpin_made, 1)
                    nc.gpsimd.tensor_tensor(cp_in[:, 1, :], ay[:, bass.ds(at + c // STEPS_IMG % 2 * HW, BLK)],
                                            x_tail[:, 1, :], ALU.add).then_inc(cpin_made, 1)
                if k == 1:
                    pool.wait_ge(nethi_made, c + 1)
                    pool.wait_ge(m1_done, 4 * c + 4)
                    nc.gpsimd.tensor_tensor(net_lo[:, :, :].rearrange("p t n -> p (t n)"),
                                            net[:, :, :].rearrange("p t n -> p (t n)"),
                                            net_hi[:, :, :].rearrange("p t n -> p (t n)").bitcast(F32),
                                            ALU.subtract).then_inc(netlo_made, 1)
                if k == 3:
                    pool.wait_ge(hidhi_made, c + 2)
                    nc.gpsimd.tensor_tensor(hid_lo[:, 2:4, :].rearrange("p t n -> p (t n)"),
                                            hid[:, 2:4, :].rearrange("p t n -> p (t n)"),
                                            hid_hi[:, 2:4, :].rearrange("p t n -> p (t n)").bitcast(F32),
                                            ALU.subtract).then_inc(hidlo_made, 1)

            def step(s, tail, last=False):
                for k in range(4):
                    if tail:
                        mlp(s - STEPS_IMG, k, s)
                    if not (last and k == 3):
                        normalise(4 * s + k + 1)
                    if not last and k % 2 == 0:
                        split_lo(2 * s + 2 + k // 2, s + 1, k // 2)

            for b in range(T):
                split_lo(b, 0, b)
            normalise(0)
            with pool.Fori(0, STEPS_IMG) as s:
                step(s, False)
            with pool.Fori(STEPS_IMG, STEPS - 1) as s:
                step(s, True)
            step(STEPS - 1, True, last=True)
            with pool.Fori(STEPS, STEPS + STEPS_IMG) as s:
                for k in range(4):
                    mlp(s - STEPS_IMG, k, None)


def kernel(**inputs):
    import numpy as np
    import concourse.bacc as bacc
    from concourse.bass_utils import run_bass_kernel_spmd

    p = {k.removeprefix("L0_conv_"): np.asarray(v) for k, v in inputs.items()}

    def columns(v):
        return v.reshape(-1, P).T

    col = np.concatenate([columns(p[n]) for n in ("xq_b", "yq_b", "xv_b", "yv_b", "xp_b", "yp_b", "cp_b", "m1_b",
                                                  "m2_b", "ls1", "ls2")], axis=1)
    w = 2 * L - 1
    rel_rows = np.stack([p["rel_x"], p["rel_y"]])[:, :, :w][:, :, ::-1]
    arrays = {
        "x": p["x"].reshape(B, DIM, HW),
        "wq": np.stack([p["xq_w"], p["yq_w"]]),
        "wk": np.stack([p["xk_w"], p["yk_w"]]),
        "wv": np.stack([p["xv_w"], p["yv_w"]]),
        "wpT": np.stack([p["xp_w"].T, p["yp_w"].T]),
        "cpT": p["cp_w"].T,
        "m1T": p["m1_w"].T,
        "m2T": p["m2_w"].T,
        "columns": col,
        "ls_rows": np.stack([p["ls1"].reshape(-1), p["ls2"].reshape(-1)]),
        "rel_tiled": np.tile(rel_rows, (1, 1, L)),
    }
    arrays = {k: np.ascontiguousarray(v) for k, v in arrays.items()}
    nc = bacc.Bacc("TRN2", target_bir_lowering=False, num_devices=1)
    args = [nc.dram_tensor(k, v.shape, mybir.dt.from_np(v.dtype), kind="ExternalInput").ap() for k, v in arrays.items()]
    o = nc.dram_tensor("out", (B, DIM, HW), F32, kind="ExternalOutput").ap()
    axial_block_kernel(nc, *args, o)
    r = run_bass_kernel_spmd(nc, [arrays], core_ids=[0])
    return r.results[0]["out"].reshape(B, DIM, L, L)
```

```python
from contextlib import ExitStack

import concourse.bass as bass
from concourse import mybir

F32 = mybir.dt.float32
F32R = mybir.dt.float32r
ALU = mybir.AluOpType
ACT = mybir.ActivationFunctionType
AX_X = mybir.AxisListType.X

P = 128
B, DIM, L = 8, 256, 56
HW = L * L
NH = 4
HALF = DIM // 2
HD = DIM // 2
SCALE = float(HD) ** -0.5
T = DIM // P
FT = 2 * DIM // P
SEQ = 4
BLK = 2 * SEQ * L
STEPS_IMG = L // (2 * SEQ)
STEPS = B * STEPS_IMG
LAST = STEPS - STEPS_IMG
LQ = L // NH
PAD = 64
QW = 2 * SEQ * L
NCOL = 30
C_QB, C_VB, C_PB, C_CPB, C_M1B, C_M2B, C_LS1, C_LS2 = 0, 8, 16, 18, 20, 24, 26, 28


def axial_block_kernel(nc, x, wq, wk, wv, wpT, cpT, m1T, m2T, columns, ls_rows, rel_tiled, out):
    ctx = ExitStack()
    with ctx:
        def sb(name, shape, dt=F32):
            return ctx.enter_context(nc.sbuf_tensor(name, shape, dt))

        def bank(name):
            return ctx.enter_context(nc.psum_tensor(name, [P, 512], F32))

        def sem(name):
            return ctx.enter_context(nc.semaphore(name))

        ident = sb("ident", [P, P])
        cols = sb("cols", [P, NCOL])
        ls_bc = sb("ls_bc", [P, 2, DIM])
        rel = sb("rel", [P, T, 2, 2, L])
        u_hi = sb("u_hi", [P, T, NH, P], F32R)
        u_lo = sb("u_lo", [P, T, NH, P], F32R)
        u_bias = sb("u_bias", [P, T, NH])
        o_w = sb("o_w", [P, T, NH, NH, P])
        o_bias = sb("o_bias", [P, T, NH])
        cp_w = sb("cp_w", [P, T, DIM])
        m1_hi = sb("m1_hi", [P, T, 2 * DIM], F32R)
        m1_lo = sb("m1_lo", [P, T, 2 * DIM], F32R)
        m2_w = sb("m2_w", [P, FT, DIM])
        m2_hi = sb("m2_hi", [P, FT, DIM], F32R)
        m2_lo = sb("m2_lo", [P, FT, DIM], F32R)
        cp_bias = sb("cp_bias", [P, T])
        m2_bias = sb("m2_bias", [P, T])
        y_image = sb("y_image", [P, 2 * HW])
        x_raw = sb("x_raw", [P, BLK])
        x_hi = sb("x_hi", [P, T, BLK], F32R)
        x_lo = sb("x_lo", [P, T, BLK], F32R)
        x_pad = sb("x_pad", [P, T, 2 * SEQ, PAD])
        u = sb("u", [P, T, 2 * SEQ, NH, PAD])
        x_t = sb("x_t", [P, 2, 2, P])
        score = sb("score", [P, QW])
        expd = sb("expd", [P, QW])
        row_max = sb("row_max", [P, 8])
        row_sum = sb("row_sum", [P, 8])
        row_rec = sb("row_rec", [P, 8])
        prob = sb("prob", [P, 8, PAD])
        prob_t = sb("prob_t", [P, 2, NH * L])
        z = sb("z", [P, NH, NH, 2 * SEQ, LQ])
        ax = sb("ax", [P, HW])
        ay = sb("ay", [P, 2 * HW])
        x_tail = sb("x_tail", [P, T, BLK])
        cp_in = sb("cp_in", [P, T, BLK])
        nets = [sb("net0", [P, T, BLK]), sb("net1", [P, T, BLK])]
        net_hi = sb("net_hi", [P, T, BLK], F32R)
        net_lo = sb("net_lo", [P, T, BLK], F32R)
        hid = sb("hid", [P, FT, BLK])
        hid_hi = sb("hid_hi", [P, FT, BLK], F32R)
        hid_lo = sb("hid_lo", [P, FT, BLK], F32R)

        stage = ay[:, 0:2 * 4 * NH * P].rearrange("p (b w h c) -> p b w h c", b=2, w=4, h=NH) \
            if 2 * HW >= 2 * 4 * NH * P else None
        st_q, st_k, st_v, st_p = (stage[:, :, w] for w in range(4))
        st_cp = ax[:, 0:T * DIM].rearrange("p (t o) -> p t o", t=T)
        st_m1 = ax[:, T * DIM:3 * T * DIM].rearrange("p (t o) -> p t o", t=T)
        st_m2 = hid[:, :, 0:DIM]

        ps_score = bank("ps_score")
        ps_pt = bank("ps_pt")
        ps_z = [bank("ps_z0"), bank("ps_z1")]
        ps_un = [bank("ps_un0"), bank("ps_un1")]
        ps_mlp = [bank("ps_mlp0"), bank("ps_mlp1")]

        ps_o = [ps_un[1], ps_score, ps_pt, ps_z[0]]

        weights_in = sem("weights_in")
        rel_in = sem("rel_in")
        rel_zeroed = sem("rel_zeroed")
        pads_zeroed = sem("pads_zeroed")
        ident_made = sem("ident_made")
        prep_mm = sem("prep_mm")
        prep_act = sem("prep_act")
        prep_dve = sem("prep_dve")
        y_loaded = sem("y_loaded")
        x_loaded = sem("x_loaded")
        tail_loaded = sem("tail_loaded")
        stored = sem("stored")
        xhi_made = sem("xhi_made")
        xlo_made = sem("xlo_made")
        xpad_made = sem("xpad_made")
        xt_done = sem("xt_done")
        xt_out = sem("xt_out")
        pt_done = sem("pt_done")
        pt_out = sem("pt_out")
        s_done = sem("s_done")
        added = sem("added")
        maxed = sem("maxed")
        shifted = sem("shifted")
        exped = sem("exped")
        summed = sem("summed")
        inverted = sem("inverted")
        prob_made = sem("prob_made")
        z_done = sem("z_done")
        z0_out = sem("z0_out")
        z1_out = sem("z1_out")
        u_done = sem("u_done")
        u_out = sem("u_out")
        o_done = sem("o_done")
        o_out = sem("o_out")
        cpin_made = sem("cpin_made")
        cp_done = sem("cp_done")
        net_made = sem("net_made")
        nethi_made = sem("nethi_made")
        netlo_made = sem("netlo_made")
        m1_done = sem("m1_done")
        hid_made = sem("hid_made")
        hidhi_made = sem("hidhi_made")
        hidlo_a_made = sem("hidlo_a_made")
        hidlo_b_made = sem("hidlo_b_made")
        m2_done = sem("m2_done")
        out_made = sem("out_made")

        x_v = x
        out_v = out

        def chunk_of(ap, c, t0, nt):
            src = ap[bass.ds(c // STEPS_IMG, 1), t0 * P:(t0 + nt) * P, bass.ds((c % STEPS_IMG) * BLK, BLK)]
            return src.rearrange("b (t p) n -> p (b t) n", p=P)

        def y_block(buf, s):
            v = buf[:, :].rearrange("p (a h w) -> p a w h", a=2, h=L)
            img, q = s // STEPS_IMG, s % STEPS_IMG
            return v[:, bass.ds(img % 2, 1), bass.ds(q * 2 * SEQ, 2 * SEQ), :].rearrange("p a w h -> p (a w) h")

        block = ctx.enter_context(nc.Block())

        @block.sync
        def _(sp):
            for b in range(T):
                for w, src in enumerate((wq, wk, wv, wpT)):
                    sp.dma_start(stage[:, b, w], src[b].rearrange("(h d) c -> d h c", d=P)).then_inc(weights_in, 16)
            sp.dma_start(st_cp, cpT.rearrange("(t p) o -> p t o", p=P)).then_inc(weights_in, 16)
            sp.dma_start(st_m1, m1T.rearrange("(t p) o -> p t o", p=P)).then_inc(weights_in, 16)
            sp.dma_start(st_m2, m2T.rearrange("(t p) o -> p t o", p=P)).then_inc(weights_in, 16)
            for q in range(STEPS_IMG):
                sp.dma_start(y_image[:, q * BLK:(q + 1) * BLK], chunk_of(x_v, q, 1, 1)[:, 0, :]).then_inc(y_loaded, 16)
            sp.dma_start(x_raw[:, :], chunk_of(x_v, 0, 0, 1)[:, 0, :]).then_inc(x_loaded, 16)

            def load_y(s):
                sp.wait_ge(xpad_made, 2 * s + 2)
                sp.wait_ge(xlo_made, 2 * s + 2)
                n = s + STEPS_IMG
                at = (n // STEPS_IMG) % 2 * HW + n % STEPS_IMG * BLK
                sp.dma_start(y_image[:, bass.ds(at, BLK)], chunk_of(x_v, n, 1, 1)[:, 0, :]).then_inc(y_loaded, 16)

            def load_x(s):
                sp.wait_ge(xpad_made, 2 * s - 1)
                sp.wait_ge(xlo_made, 2 * s - 1)
                sp.dma_start(x_raw[:, :], chunk_of(x_v, s, 0, 1)[:, 0, :]).then_inc(x_loaded, 16)

            def load_tail(c):
                sp.dma_start(x_tail[:, :, :], chunk_of(x_v, c, 0, T)).then_inc(tail_loaded, 16)

            def step(s, y=False, xr=False, tail=False, more=False):
                c = s - STEPS_IMG
                if y:
                    load_y(s)
                if more:
                    sp.wait_ge(net_made, 2 * c + 2)
                    load_tail(c + 1)
                if xr:
                    load_x(s + 2)
                if tail:
                    sp.wait_ge(out_made, 2 * c + 4)
                    sp.dma_start(chunk_of(out_v, c, 0, T), nets[0][:, :, :]).then_inc(stored, 16)

            def last_image(c, buf, more=True):
                if more:
                    sp.wait_ge(net_made, 2 * c + 4)
                    load_tail(c + 2)
                sp.wait_ge(out_made, 2 * c + 4)
                sp.dma_start(chunk_of(out_v, c, 0, T), nets[buf][:, :, :]).then_inc(stored, 16)

            load_x(1)
            with sp.Fori(0, STEPS_IMG) as s:
                step(s, y=True, xr=True)
            load_tail(0)
            with sp.Fori(STEPS_IMG, STEPS - STEPS_IMG) as s:
                step(s, y=True, xr=True, tail=True, more=True)
            with sp.Fori(STEPS - STEPS_IMG, STEPS - 2) as s:
                step(s, xr=True, tail=True, more=True)
            for s in range(STEPS - 2, STEPS):
                step(s, tail=True, more=True)
            sp.wait_ge(net_made, 2 * LAST + 2)
            load_tail(LAST + 1)
            with sp.Fori(LAST, STEPS - 3, 2) as c:
                last_image(c, 0)
                last_image(c + 1, 1)
            last_image(STEPS - 3, 0)
            last_image(STEPS - 2, 1, more=False)
            last_image(STEPS - 1, 0, more=False)
            sp.wait_ge(stored, 16 * (STEPS + 1))

        @block.tensor
        def _(pe):
            mm = nc.tensor.matmul

            pe.wait_ge(weights_in, 16 * 11)
            pe.wait_ge(rel_in, 16 * (1 + 2 * T * NH + 2))
            for b in range(T):
                if b == 1:
                    pe.wait_ge(prep_act, 1)
                    pe.wait_ge(prep_dve, 7)
                for h in range(NH):
                    mm(ps_un[0][:, h * P:(h + 1) * P], st_q[:, b, h], st_k[:, b, h], start=True, stop=True)
                    mm(ps_o[h][:, :], st_v[:, b, h], st_p[:, b].rearrange("p m o -> p (m o)"), start=True, stop=True)
                for h in range(NH):
                    mm(ps_mlp[0][:, h:h + 1], st_k[:, b, h], cols[:, C_QB + b * NH + h:C_QB + b * NH + h + 1],
                       start=True, stop=True)
                for m in range(NH):
                    last = mm(ps_mlp[1][:, 0:NH], st_p[:, b, m], cols[:, C_VB + b * NH:C_VB + (b + 1) * NH],
                              start=(m == 0), stop=(m == NH - 1))
                last.then_inc(prep_mm, 1)
            pe.sem_inc(s_done, 2)
            pe.sem_inc(z_done, 1)
            pe.sem_inc(o_done, 1)
            pe.sem_inc(cp_done, 2)
            pe.sem_inc(m1_done, 4)
            pe.sem_inc(m2_done, 2)
            pe.wait_ge(ident_made, 2)
            pe.wait_ge(pads_zeroed, 3)
            pe.wait_ge(prep_act, 2)
            pe.wait_ge(prep_dve, 19)

            def three(ps, w_hi, w_lo, a_hi, a_lo, first, last):
                mm(ps, w_lo, a_hi, start=first, stop=False)
                mm(ps, w_hi, a_lo, start=False, stop=False)
                return mm(ps, w_hi, a_hi, start=False, stop=last)

            def values_t(g, k):
                br, kk = k // 2, k % 2
                pe.wait_ge(xpad_made, g // 2 + 1 if isinstance(g, int) else 2 * ((g - k) // 4) + br + 1)
                if not isinstance(g, int) or g:
                    pe.wait_ge(z0_out, g)
                    pe.wait_ge(xt_out, g)
                for pair in range(2):
                    last = nc.tensor.transpose(ps_z[0][:, pair * P:(pair + 1) * P],
                                               x_pad[:, br, 4 * kk + 2 * pair:4 * kk + 2 * pair + 2, :]
                                               .rearrange("p s i -> p (s i)"), ident[:, :])
                last.then_inc(xt_done, 1)

            def scores(g, blk, k):
                br, kk = k // 2, k % 2
                pe.wait_ge(u_out, 4 * blk + 4)
                if not isinstance(g, int) or g:
                    pe.wait_ge(added, g)
                for pair in range(2):
                    for hp in range(2):
                        for sq in range(2):
                            n = 4 * kk + 2 * pair + sq
                            at = ((pair * 2 + hp) * 2 + sq) * L
                            last = mm(ps_score[:, at:at + L],
                                      u[:, br, n, 2 * hp:2 * hp + 2, :].rearrange("p h i -> p (h i)"),
                                      x_pad[:, br, n, 0:L], start=True, stop=True)
                last.then_inc(s_done, 1)

            def probs_t(g):
                pe.wait_ge(prob_made, g + 1)
                pe.wait_ge(pt_out, g + 1)
                for n in range(4):
                    last = nc.tensor.transpose(ps_pt[:, n * P:(n + 1) * P],
                                               prob[:, 2 * n:2 * n + 2, :].rearrange("p s j -> p (s j)"),
                                               ident[:, :])
                last.then_inc(pt_done, 1)

            def weigh(g, k, more):
                pe.wait_ge(pt_out, g + 2)
                pe.wait_ge(xt_out, g + 2 if more else g + 1)
                pe.wait_ge(z1_out, g + 1)
                pe.wait_ge(z0_out, g + 1)
                for pair in range(2):
                    for sq in range(2):
                        rows = slice(PAD * sq, PAD * sq + L)
                        last = mm(ps_z[sq][:, pair * NH * L:(pair + 1) * NH * L], x_t[rows, k % 2, pair, :],
                                  prob_t[rows, pair, :], start=True, stop=True)
                last.then_inc(z_done, 1)

            def queries(m, blk, h, bk, free):
                br = h[1]
                pe.wait_ge(xhi_made, blk + 1)
                pe.wait_ge(xlo_made, blk + 1)
                if free is not None:
                    pe.wait_ge(*free)
                three(ps_un[bk][:, 0:BLK], u_hi[:, br, h[0]], u_lo[:, br, h[0]], x_hi[:, br, :], x_lo[:, br, :],
                      True, True).then_inc(u_done, 1)

            def project(blk, br, g, bk, free):
                pe.wait_ge(z0_out, g + 2)
                pe.wait_ge(z1_out, g + 2)
                pe.wait_ge(*free)
                n = BLK // NH
                for h in range(NH):
                    for m in range(NH):
                        last = mm(ps_un[bk][:, h * n:(h + 1) * n], o_w[:, br, h, m],
                                  z[:, h, m].rearrange("p s i -> p (s i)"), start=(m == 0), stop=(m == NH - 1))
                last.then_inc(o_done, 1)

            def compress(c, first=True):
                for t in range(T):
                    pe.wait_ge(cpin_made, 2 * c + 2)
                    if first:
                        pe.wait_ge(out_made, 2 * c + 1 + t)
                    else:
                        pe.wait_ge(hid_made, 4 * c - 1 + t)
                    for i in range(T):
                        last = mm(ps_mlp[t][:, 0:BLK], cp_w[:, i, t * P:(t + 1) * P], cp_in[:, i, :],
                                  start=(i == 0), stop=(i == T - 1))
                    last.then_inc(cp_done, 1)

            def expand(c, t, first=True):
                pe.wait_ge(nethi_made, c + 1)
                pe.wait_ge(netlo_made, c + 1)
                if t >= 2:
                    pe.wait_ge(hid_made, 4 * c + t - 1)
                elif first:
                    pe.wait_ge(net_made, 2 * c + 1 + t)
                else:
                    pe.wait_ge(out_made, 2 * c + 1 + t)
                for i in range(T):
                    last = three(ps_mlp[t % 2][:, 0:BLK], m1_hi[:, i, t * P:(t + 1) * P],
                                 m1_lo[:, i, t * P:(t + 1) * P], net_hi[:, i, :], net_lo[:, i, :],
                                 i == 0, i == T - 1)
                last.then_inc(m1_done, 1)

            def contract(c, first=True):
                for t in range(T):
                    if first:
                        pe.wait_ge(hid_made, 4 * c + 3 + t)
                    else:
                        pe.wait_ge(net_made, 2 * c + 3 + t)
                    for i in range(FT):
                        if t == 0 and i % 2 == 0:
                            pe.wait_ge(hidhi_made, 2 * c + 3 + i // 2)
                            pe.wait_ge(hidlo_a_made if i == 0 else hidlo_b_made, c + 2)
                        last = three(ps_mlp[t][:, 0:BLK], m2_hi[:, i, t * P:(t + 1) * P],
                                     m2_lo[:, i, t * P:(t + 1) * P], hid_hi[:, i, :], hid_lo[:, i, :],
                                     i == 0, i == FT - 1)
                    last.then_inc(m2_done, 1)

            jobs = [("u", 0), ("u", 1), ("u", 2), ("u", 3), ("o", 0), ("u", 4), ("u", 5), ("u", 6), ("u", 7), ("o", 1)]

            def freed(s, n, emitted):
                for j in range(n - 2, -1, -2):
                    kind, i = jobs[j]
                    if kind == "o":
                        return o_out, 2 * s + i + 3
                    if i in emitted:
                        return u_out, 8 * s + 6 + i + 1
                return (u_out, 8 * s + 6) if n == 0 or n == 1 and isinstance(s, int) and s == 0 else (o_out, 2 * s + 2)

            def step(s, tail, last=False):
                emitted = set()
                n = 0
                for k in range(4):
                    g = 4 * s + k
                    more = not (last and k == 3)
                    if more:
                        values_t(g + 1, (k + 1) % 4)
                    probs_t(g)
                    if more:
                        scores(g + 1, 2 * s + (k + 1) // 2, (k + 1) % 4)
                    weigh(g, k, more)
                    c = s - STEPS_IMG
                    if tail and k == 1:
                        expand(c, 0)
                        expand(c, 1)
                    for hh in range(2):
                        if not (last and k > 0):
                            head = 2 * ((k + 3) % 2) + hh
                            blk = 2 * s + (k + 3) // 2
                            queries(None, blk, (head, (k + 3) // 2 % 2), n % 2, freed(s, n, emitted))
                            emitted.add(2 * k + hh)
                        n += 1
                    if tail and k == 0:
                        compress(c)
                    if tail and k == 1:
                        expand(c, 2)
                        expand(c, 3)
                    if tail and k == 3:
                        contract(c)
                    if k % 2:
                        project(2 * s + k // 2, k // 2, g, n % 2, freed(s, n, emitted))
                        n += 1

            for m in range(6):
                queries(m, m // 4, (m % 4, m // 4), m % 2, (u_out, m - 1) if m >= 2 else None)
            values_t(0, 0)
            scores(0, 0, 0)
            with pe.Fori(0, STEPS_IMG) as s:
                step(s, False)
            with pe.Fori(STEPS_IMG, STEPS - 1) as s:
                step(s, True)
            step(STEPS - 1, True, last=True)

            def last_image(c, more=True):
                for t in range(FT):
                    expand(c, t, first=isinstance(c, int) and c == LAST)
                if more:
                    compress(c + 1, first=False)
                contract(c, first=not more)

            compress(LAST)
            last_image(LAST)
            with pe.Fori(LAST + 1, STEPS - 1) as c:
                last_image(c)
            last_image(STEPS - 1, more=False)

        @block.scalar
        def _(act):
            act.dma_start(cols[:, :], columns).then_inc(rel_in, 16)
            for n in range(2):
                act.dma_start(ls_bc[:, n, :], ls_rows[n:n + 1, :].to_broadcast([P, DIM])).then_inc(rel_in, 16)
            act.wait_ge(rel_zeroed, 1)
            for b in range(T):
                for h in range(NH):
                    w = 2 * L - 1
                    src = rel_tiled[b, h, L - 1:L - 1 + L * (w - 1)].rearrange("(i j) -> i j", j=w - 1)[:, 0:L]
                    for sq in range(2):
                        act.dma_start(rel[PAD * (h % 2):PAD * (h % 2) + L, b, h // 2, sq, :], src).then_inc(rel_in, 16)
            for b in range(T):
                act.wait_ge(prep_mm, b + 1)
                nc.scalar.activation(u_hi[:, b].rearrange("p h c -> p (h c)"), ps_un[0][:, :], ACT.Copy,
                                     scale=SCALE).then_inc(prep_act, 1)
                if b == 0:
                    act.wait_ge(prep_dve, 1)
            act.sem_inc(pt_out, 1)
            act.sem_inc(z1_out, 1)

            def query_out(m, blk, h, br):
                act.wait_ge(u_done, m + 1)
                if not isinstance(m, int) or blk:
                    act.wait_ge(s_done, 2 * blk)
                nc.scalar.activation(u[:, br, :, h, 0:L], ps_un[m % 2 if isinstance(m, int) else bank_of[0]][:, 0:BLK]
                                     .rearrange("p (s i) -> p s i", i=L), ACT.Identity,
                                     bias=u_bias[:, br, h:h + 1]).then_inc(u_out, 1)

            bank_of = [0]

            def exps(g):
                act.wait_ge(shifted, g + 1)
                if not isinstance(g, int) or g:
                    act.wait_ge(prob_made, g)
                nc.scalar.activation(expd[:, :], score[:, :], ACT.Exp).then_inc(exped, 1)

            def step(s, tail, last=False):
                n = 0
                c = s - STEPS_IMG
                for k in range(4):
                    g = 4 * s + k
                    act.wait_ge(pt_done, g + 1)
                    act.wait_ge(z_done, g + 1)
                    nc.scalar.activation(prob_t[:, :, :].rearrange("p a (h m i) -> p (a h) m i", m=NH, i=LQ),
                                         ps_pt[:, :].rearrange("p (n i m) -> p n m i", i=PAD // NH, m=NH)[:, :, :, 0:LQ],
                                         ACT.Copy).then_inc(pt_out, 1)
                    if not (last and k == 3):
                        exps(g + 1)
                    act.wait_ge(z_done, g + 2)
                    if k % 2 == 0:
                        act.wait_ge(o_done, 2 * s + k // 2 + 1)
                    take_z(nc.scalar, 1, k).then_inc(z1_out, 1)
                    if tail and k == 1:
                        hidden(c, 0)
                        hidden(c, 1)
                    for hh in range(2):
                        if not (last and k > 0):
                            bank_of[0] = n % 2
                            query_out(8 * s + 2 * k + 6 + hh, 2 * s + (k + 3) // 2, 2 * ((k + 3) % 2) + hh,
                                      (k + 3) // 2 % 2)
                        n += 1
                    n += k % 2
                    if tail and k == 0:
                        split_net(c, 0)
                    if tail and k == 1:
                        hidden(c, 2)
                        hidden(c, 3)

            def take_z(eng, sq, k):
                src = ps_z[sq][:, 0:2 * NH * L].rearrange("p (a n i) -> p a n i", a=2, i=LQ)
                dst = z[:, :, :, :, :].rearrange("p h m (q a s) i -> p q s a (h m) i", q=2, a=2)[:, k % 2, sq]
                return eng.activation(dst, src, ACT.Copy)

            def split_net(c, buf):
                act.wait_ge(net_made, 2 * c + 2)
                act.wait_ge(m1_done, 4 * c + 4)
                nc.scalar.activation(net_hi[:, :, :].rearrange("p t n -> p (t n)"),
                                     nets[buf][:, :, :].rearrange("p t n -> p (t n)"), ACT.Copy).then_inc(nethi_made, 1)

            def hidden(c, t):
                if t == 0:
                    act.wait_ge(hidhi_made, 2 * c + 2)
                    act.wait_ge(hidlo_a_made, c + 1)
                    act.wait_ge(hidlo_b_made, c + 1)
                act.wait_ge(m1_done, 4 * c + t + 5)
                nc.scalar.activation(hid[:, t, :], ps_mlp[t % 2][:, 0:BLK], ACT.Gelu,
                                     bias=cols[:, C_M1B + t:C_M1B + t + 1]).then_inc(hid_made, 1)

            act.wait_ge(prep_dve, 19)
            act.wait_ge(pads_zeroed, 3)
            for m in range(6):
                query_out(m, m // 4, m % 4, m // 4)
            exps(0)
            with act.Fori(0, STEPS_IMG) as s:
                step(s, False)
            with act.Fori(STEPS_IMG, STEPS - 1) as s:
                step(s, True)
            step(STEPS - 1, True, last=True)

            def last_image(c, buf, more=True):
                for t in range(FT):
                    hidden(c, t)
                if more:
                    split_net(c + 1, 1 - buf)

            split_net(LAST, 0)
            with act.Fori(LAST, STEPS - 1, 2) as c:
                last_image(c, 0)
                last_image(c + 1, 1)
            last_image(STEPS - 1, 0, more=False)

        @block.vector
        def _(dve):
            nc.vector.memset(rel[:, :, :, :, :], 0.0).then_inc(rel_zeroed, 1)
            nc.vector.memset(x_pad[:, :, :, :], 0.0).then_inc(pads_zeroed, 1)
            nc.vector.memset(u[:, :, :, :, :], 0.0).then_inc(pads_zeroed, 1)
            nc.vector.memset(prob[:, :, :], 0.0).then_inc(pads_zeroed, 1)
            dve.wait_ge(weights_in, 16 * 11)
            dve.wait_ge(rel_in, 16 * (1 + 2 * T * NH + 2))
            dve.wait_ge(prep_mm, 1)
            for b in range(T):
                if b:
                    dve.wait_ge(prep_mm, 2)
                dve.wait_ge(prep_act, b + 1)
                nc.vector.scalar_tensor_tensor(out=u_lo[:, b].rearrange("p h c -> p (h c)"), in0=ps_un[0][:, :],
                                               scalar=SCALE, in1=u_hi[:, b].rearrange("p h c -> p (h c)").bitcast(F32),
                                               op0=ALU.mult, op1=ALU.subtract).then_inc(prep_dve, 1)
                for h in range(NH):
                    nc.vector.tensor_copy(o_w[:, b, h].rearrange("p m o -> p (m o)"), ps_o[h][:, :]).then_inc(prep_dve, 1)
                nc.vector.tensor_scalar(u_bias[:, b, :], ps_mlp[0][:, 0:NH], SCALE, None, ALU.mult).then_inc(prep_dve, 1)
                nc.vector.tensor_scalar(o_bias[:, b, :], ps_mlp[1][:, 0:NH], cols[:, C_PB + b:C_PB + b + 1], None,
                                        ALU.add).then_inc(prep_dve, 1)
            for i in range(T):
                nc.vector.tensor_tensor(cp_w[:, i, :], st_cp[:, i, :], ls_bc[:, 0, :], ALU.mult)
            nc.vector.tensor_tensor(cp_bias[:, :], cols[:, C_CPB:C_CPB + T], cols[:, C_LS1:C_LS1 + T], ALU.mult)
            nc.vector.tensor_tensor(m2_bias[:, :], cols[:, C_M2B:C_M2B + T], cols[:, C_LS2:C_LS2 + T], ALU.mult)
            for i in range(FT):
                last = nc.vector.tensor_tensor(m2_w[:, i, :], st_m2[:, i, :], ls_bc[:, 1, :], ALU.mult)
            last.then_inc(prep_dve, 1)
            nc.vector.tensor_copy(m1_hi[:, :, :].rearrange("p t o -> p (t o)"),
                                  st_m1.rearrange("p t o -> p (t o)")).then_inc(prep_dve, 1)
            dve.wait_ge(prep_dve, 15)
            nc.vector.tensor_copy(m2_hi[:, :, :].rearrange("p t o -> p (t o)"),
                                  m2_w[:, :, :].rearrange("p t o -> p (t o)")).then_inc(prep_dve, 1)
            dve.wait_ge(prep_dve, 16)
            nc.vector.tensor_tensor(m1_lo[:, :, :].rearrange("p t o -> p (t o)"), st_m1.rearrange("p t o -> p (t o)"),
                                    m1_hi[:, :, :].rearrange("p t o -> p (t o)").bitcast(F32),
                                    ALU.subtract).then_inc(prep_dve, 1)
            dve.wait_ge(prep_dve, 17)
            nc.vector.tensor_tensor(m2_lo[:, :, :].rearrange("p t o -> p (t o)"),
                                    m2_w[:, :, :].rearrange("p t o -> p (t o)"),
                                    m2_hi[:, :, :].rearrange("p t o -> p (t o)").bitcast(F32),
                                    ALU.subtract).then_inc(prep_dve, 1)
            dve.wait_ge(prep_dve, 19)
            dve.wait_ge(pads_zeroed, 3)
            dve.sem_inc(z0_out, 1)
            dve.sem_inc(o_out, 2)
            dve.sem_inc(hidhi_made, 2)
            dve.sem_inc(hidlo_a_made, 1)
            dve.sem_inc(out_made, 2)
            dve.sem_inc(stored, 16)

            def split_hi(blk, s, br):
                if br == 0:
                    dve.wait_ge(x_loaded, 16 * s + 16)
                    src = x_raw[:, :].rearrange("p (s i) -> p s i", i=L)
                else:
                    dve.wait_ge(y_loaded, 16 * STEPS_IMG * (s // STEPS_IMG + 1))
                    src = y_block(y_image, s)
                if not isinstance(blk, int) or blk >= 2:
                    dve.wait_ge(u_done, 4 * blk - 4)
                nc.vector.tensor_scalar(x_hi[:, br, :].rearrange("p (s i) -> p s i", i=L), src, 1.0, None,
                                        ALU.mult).then_inc(xhi_made, 1)

            def pad(blk, s, br):
                src = x_raw[:, :].rearrange("p (s i) -> p s i", i=L) if br == 0 else y_block(y_image, s)
                if not isinstance(blk, int) or blk >= 2:
                    dve.wait_ge(s_done, 2 * blk)
                    dve.wait_ge(xt_done, 2 * blk - 2)
                nc.vector.tensor_scalar(x_pad[:, br, :, 0:L], src, 1.0, None, ALU.mult).then_inc(xpad_made, 1)

            def softmax_a(g, k):
                br = k // 2
                dve.wait_ge(s_done, g + 3)
                if not isinstance(g, int) or g:
                    dve.wait_ge(exped, g)
                nc.vector.tensor_tensor(score[:, :].rearrange("p (a n) -> p a n", a=2),
                                        ps_score[:, 0:QW].rearrange("p (a n) -> p a n", a=2),
                                        rel[:, br].rearrange("p h s j -> p (h s j)").unsqueeze(1)
                                        .to_broadcast([P, 2, QW // 2]), ALU.add).then_inc(added, 1)
                rows = score[:, :].rearrange("p (n j) -> p n j", j=L)
                dve.wait_ge(added, g + 1)
                nc.vector.tensor_reduce(row_max[:, :], rows, AX_X, ALU.max).then_inc(maxed, 1)
                dve.wait_ge(maxed, g + 1)
                nc.vector.tensor_tensor(rows, rows, row_max[:, :].unsqueeze(2).to_broadcast([P, 8, L]),
                                        ALU.subtract).then_inc(shifted, 1)

            def softmax_b(g):
                dve.wait_ge(exped, g + 1)
                nc.vector.tensor_reduce(row_sum[:, :], expd[:, :].rearrange("p (n j) -> p n j", j=L), AX_X,
                                        ALU.add).then_inc(summed, 1)
                dve.wait_ge(summed, g + 1)
                if not isinstance(g, int) or g:
                    dve.wait_ge(prob_made, g)
                nc.vector.reciprocal(row_rec[:, :], row_sum[:, :]).then_inc(inverted, 1)

            def values_out(g, k):
                dve.wait_ge(xt_done, g + 1)
                if not isinstance(g, int) or g:
                    dve.wait_ge(z_done, g)
                nc.vector.tensor_copy(x_t[:, k % 2].rearrange("p a c -> p (a c)"),
                                      ps_z[0][:, 0:2 * P]).then_inc(xt_out, 1)

            def step(s, tail, last=False):
                c = s - STEPS_IMG
                for k in range(4):
                    g = 4 * s + k
                    more = not (last and k == 3)
                    if more:
                        values_out(g + 1, (k + 1) % 4)
                        softmax_a(g + 1, (k + 1) % 4)
                    dve.wait_ge(z_done, g + 2)
                    if k % 2 == 0:
                        dve.wait_ge(o_done, 2 * s + k // 2 + 1)
                    src = ps_z[0][:, 0:2 * NH * L].rearrange("p (a n i) -> p a n i", a=2, i=LQ)
                    dst = z[:, :, :, :, :].rearrange("p h m (q a s) i -> p q s a (h m) i", q=2, a=2)[:, k % 2, 0]
                    nc.vector.tensor_copy(dst, src).then_inc(z0_out, 1)
                    if more:
                        softmax_b(g + 1)
                    if not last:
                        if k % 2 == 0:
                            split_hi(2 * s + 2 + k // 2, s + 1, k // 2)
                        else:
                            pad(2 * s + 2 + k // 2, s + 1, k // 2)
                    if tail and k == 0:
                        add_net(c, 0, 16 * c + 16)
                    if tail and k == 1:
                        split_hidden(c)
                    if tail and k == 3:
                        add_out(c, 0)
                    if k % 2:
                        dve.wait_ge(o_done, 2 * s + k // 2 + 2)
                        if tail:
                            dve.wait_ge(cpin_made, 2 * c + 2)
                        src = ps_un[(4 if k == 1 else 9) % 2][:, 0:BLK].rearrange("p (n s i) -> p n s i", n=NH, i=LQ)
                        if k == 1:
                            dst = ax[:, bass.ds(s % STEPS_IMG * BLK, BLK)].rearrange("p (s n i) -> p n s i", n=NH, i=LQ)
                        else:
                            dst = y_block(ay, s).rearrange("p s (n i) -> p n s i", n=NH)
                        bias = o_bias[:, k // 2, :].unsqueeze(2).unsqueeze(3).to_broadcast([P, NH, 2 * SEQ, LQ])
                        nc.vector.tensor_tensor(dst, src, bias, ALU.add).then_inc(o_out, 1)

            def add_net(c, buf, free):
                for t in range(T):
                    dve.wait_ge(cp_done, 2 * c + t + 3)
                    dve.wait_ge(stored, free)
                    dve.wait_ge(tail_loaded, 16 * c + 16)
                    nc.vector.scalar_tensor_tensor(out=nets[buf][:, t, :], in0=ps_mlp[t][:, 0:BLK],
                                                   scalar=cp_bias[:, t:t + 1], in1=x_tail[:, t, :],
                                                   op0=ALU.add, op1=ALU.add).then_inc(net_made, 1)

            def split_hidden(c):
                dve.wait_ge(m2_done, 2 * c + 2)
                for t in (0, 2):
                    dve.wait_ge(hid_made, 4 * c + t + 2)
                    nc.vector.tensor_copy(hid_hi[:, t:t + 2, :].rearrange("p t n -> p (t n)"),
                                          hid[:, t:t + 2, :].rearrange("p t n -> p (t n)")).then_inc(hidhi_made, 1)
                dve.wait_ge(hidhi_made, 2 * c + 3)
                nc.vector.tensor_tensor(hid_lo[:, 0:2, :].rearrange("p t n -> p (t n)"),
                                        hid[:, 0:2, :].rearrange("p t n -> p (t n)"),
                                        hid_hi[:, 0:2, :].rearrange("p t n -> p (t n)").bitcast(F32),
                                        ALU.subtract).then_inc(hidlo_a_made, 1)

            def add_out(c, buf):
                for t in range(T):
                    dve.wait_ge(m2_done, 2 * c + t + 3)
                    nc.vector.scalar_tensor_tensor(out=nets[buf][:, t, :], in0=ps_mlp[t][:, 0:BLK],
                                                   scalar=m2_bias[:, t:t + 1], in1=nets[buf][:, t, :],
                                                   op0=ALU.add, op1=ALU.add).then_inc(out_made, 1)

            for b in range(T):
                split_hi(b, 0, b)
                pad(b, 0, b)
            values_out(0, 0)
            softmax_a(0, 0)
            softmax_b(0)
            with dve.Fori(0, STEPS_IMG) as s:
                step(s, False)
            with dve.Fori(STEPS_IMG, STEPS - 1) as s:
                step(s, True)
            step(STEPS - 1, True, last=True)

            def last_image(c, buf, more=True):
                split_hidden(c)
                if more:
                    add_net(c + 1, 1 - buf, 16 * c + 16)
                add_out(c, buf)

            add_net(LAST, 0, 16 * LAST + 16)
            with dve.Fori(LAST, STEPS - 1, 2) as c:
                last_image(c, 0)
                last_image(c + 1, 1)
            last_image(STEPS - 1, 0, more=False)

        @block.gpsimd
        def _(pool):
            nc.gpsimd.memset(ident[:, :], 0.0).then_inc(ident_made, 1)
            pool.wait_ge(ident_made, 1)
            nc.gpsimd.affine_select(out=ident[:, :], in_=ident[:, :], compare_op=ALU.not_equal, fill=1.0, base=0,
                                    pattern=[[-1, P]], channel_multiplier=1).then_inc(ident_made, 1)

            pool.wait_ge(pads_zeroed, 3)

            def split_lo(blk, s, br):
                pool.wait_ge(xhi_made, blk + 1)
                pool.wait_ge(ident_made, 2)
                src = x_raw[:, :].rearrange("p (s i) -> p s i", i=L) if br == 0 else y_block(y_image, s)
                nc.gpsimd.tensor_tensor(x_lo[:, br, :].rearrange("p (s i) -> p s i", i=L), src,
                                        x_hi[:, br, :].rearrange("p (s i) -> p s i", i=L).bitcast(F32),
                                        ALU.subtract).then_inc(xlo_made, 1)

            def normalise(g):
                pool.wait_ge(inverted, g + 1)
                if not isinstance(g, int) or g:
                    pool.wait_ge(pt_done, g)
                nc.gpsimd.tensor_tensor(prob[:, :, 0:L], expd[:, :].rearrange("p (n j) -> p n j", j=L),
                                        row_rec[:, :].unsqueeze(2).to_broadcast([P, 8, L]),
                                        ALU.mult).then_inc(prob_made, 1)

            def add_input(c):
                pool.wait_ge(o_out, 2 * (STEPS_IMG * (c // STEPS_IMG) + STEPS_IMG) + 2)
                pool.wait_ge(tail_loaded, 16 * c + 16)
                pool.wait_ge(cp_done, 2 * c + 2)
                pool.wait_ge(ident_made, 2)
                at = c % STEPS_IMG * BLK
                nc.gpsimd.tensor_tensor(cp_in[:, 0, :], ax[:, bass.ds(at, BLK)], x_tail[:, 0, :],
                                        ALU.add).then_inc(cpin_made, 1)
                nc.gpsimd.tensor_tensor(cp_in[:, 1, :], ay[:, bass.ds(at + c // STEPS_IMG % 2 * HW, BLK)],
                                        x_tail[:, 1, :], ALU.add).then_inc(cpin_made, 1)

            def split_net(c, buf):
                pool.wait_ge(nethi_made, c + 1)
                pool.wait_ge(m1_done, 4 * c + 4)
                nc.gpsimd.tensor_tensor(net_lo[:, :, :].rearrange("p t n -> p (t n)"),
                                        nets[buf][:, :, :].rearrange("p t n -> p (t n)"),
                                        net_hi[:, :, :].rearrange("p t n -> p (t n)").bitcast(F32),
                                        ALU.subtract).then_inc(netlo_made, 1)

            def split_hidden(c):
                pool.wait_ge(hidhi_made, 2 * c + 4)
                nc.gpsimd.tensor_tensor(hid_lo[:, 2:4, :].rearrange("p t n -> p (t n)"),
                                        hid[:, 2:4, :].rearrange("p t n -> p (t n)"),
                                        hid_hi[:, 2:4, :].rearrange("p t n -> p (t n)").bitcast(F32),
                                        ALU.subtract).then_inc(hidlo_b_made, 1)

            def step(s, tail, last=False):
                c = s - STEPS_IMG
                for k in range(4):
                    if tail and k == 0:
                        add_input(c)
                    if tail and k == 1:
                        split_net(c, 0)
                    if tail and k == 2:
                        split_hidden(c)
                    if not (last and k == 3):
                        normalise(4 * s + k + 1)
                    if not last and k % 2 == 0:
                        split_lo(2 * s + 2 + k // 2, s + 1, k // 2)

            pool.sem_inc(hidlo_b_made, 1)
            for b in range(T):
                split_lo(b, 0, b)
            normalise(0)
            with pool.Fori(0, STEPS_IMG) as s:
                step(s, False)
            with pool.Fori(STEPS_IMG, STEPS - 1) as s:
                step(s, True)
            step(STEPS - 1, True, last=True)

            def last_image(c, buf, more=True):
                if more:
                    add_input(c + 1)
                split_hidden(c)
                if more:
                    split_net(c + 1, 1 - buf)

            add_input(LAST)
            split_net(LAST, 0)
            with pool.Fori(LAST, STEPS - 1, 2) as c:
                last_image(c, 0)
                last_image(c + 1, 1)
            last_image(STEPS - 1, 0, more=False)


def kernel(**inputs):
    import numpy as np
    import concourse.bacc as bacc
    from concourse.bass_utils import run_bass_kernel_spmd

    p = {k.removeprefix("L0_conv_"): np.asarray(v) for k, v in inputs.items()}

    def columns(v):
        return v.reshape(-1, P).T

    col = np.concatenate([columns(p[n]) for n in ("xq_b", "yq_b", "xv_b", "yv_b", "xp_b", "yp_b", "cp_b", "m1_b",
                                                  "m2_b", "ls1", "ls2")], axis=1)
    w = 2 * L - 1
    rel_rows = np.stack([p["rel_x"], p["rel_y"]])[:, :, :w][:, :, ::-1]
    arrays = {
        "x": p["x"].reshape(B, DIM, HW),
        "wq": np.stack([p["xq_w"], p["yq_w"]]),
        "wk": np.stack([p["xk_w"], p["yk_w"]]),
        "wv": np.stack([p["xv_w"], p["yv_w"]]),
        "wpT": np.stack([p["xp_w"].T, p["yp_w"].T]),
        "cpT": p["cp_w"].T,
        "m1T": p["m1_w"].T,
        "m2T": p["m2_w"].T,
        "columns": col,
        "ls_rows": np.stack([p["ls1"].reshape(-1), p["ls2"].reshape(-1)]),
        "rel_tiled": np.tile(rel_rows, (1, 1, L)),
    }
    arrays = {k: np.ascontiguousarray(v) for k, v in arrays.items()}
    nc = bacc.Bacc("TRN2", target_bir_lowering=False, num_devices=1)
    args = [nc.dram_tensor(k, v.shape, mybir.dt.from_np(v.dtype), kind="ExternalInput").ap() for k, v in arrays.items()]
    o = nc.dram_tensor("out", (B, DIM, HW), F32, kind="ExternalOutput").ap()
    axial_block_kernel(nc, *args, o)
    r = run_bass_kernel_spmd(nc, [arrays], core_ids=[0])
    return r.results[0]["out"].reshape(B, DIM, L, L)
```

```python
from contextlib import ExitStack

import concourse.bass as bass
from concourse import mybir

F32 = mybir.dt.float32
F32R = mybir.dt.float32r
ALU = mybir.AluOpType
ACT = mybir.ActivationFunctionType
AX_X = mybir.AxisListType.X

P = 128
B, DIM, L = 8, 256, 56
HW = L * L
NH = 4
HALF = DIM // 2
HD = DIM // 2
SCALE = float(HD) ** -0.5
T = DIM // P
FT = 2 * DIM // P
SEQ = 4
BLK = 2 * SEQ * L
STEPS_IMG = L // (2 * SEQ)
STEPS = B * STEPS_IMG
LAST = STEPS - STEPS_IMG
LQ = L // NH
PAD = 64
QR = 2 * L
QW = 2 * SEQ * L
NCOL = 30
C_QB, C_VB, C_PB, C_CPB, C_M1B, C_M2B, C_LS1, C_LS2 = 0, 8, 16, 18, 20, 24, 26, 28


def axial_block_kernel(nc, x, wq, wk, wv, wpT, cpT, m1T, m2T, columns, ls_rows, rel_tiled, out):
    ctx = ExitStack()
    with ctx:
        def sb(name, shape, dt=F32):
            return ctx.enter_context(nc.sbuf_tensor(name, shape, dt))

        def bank(name):
            return ctx.enter_context(nc.psum_tensor(name, [P, 512], F32))

        def sem(name):
            return ctx.enter_context(nc.semaphore(name))

        ident = sb("ident", [P, P])
        cols = sb("cols", [P, NCOL])
        ls_bc = sb("ls_bc", [P, 2, DIM])
        rel = sb("rel", [QR, T, 2, L])
        u_hi = sb("u_hi", [P, T, NH, P], F32R)
        u_lo = sb("u_lo", [P, T, NH, P], F32R)
        u_bias = sb("u_bias", [P, T, NH])
        o_w = sb("o_w", [P, T, NH, NH, P])
        o_bias = sb("o_bias", [P, T, NH])
        cp_hi = sb("cp_hi", [P, T, DIM], F32R)
        cp_lo = sb("cp_lo", [P, T, DIM], F32R)
        m1_hi = sb("m1_hi", [P, T, 2 * DIM], F32R)
        m1_lo = sb("m1_lo", [P, T, 2 * DIM], F32R)
        m2_hi = sb("m2_hi", [P, FT, DIM], F32R)
        m2_lo = sb("m2_lo", [P, FT, DIM], F32R)
        cp_bias = sb("cp_bias", [P, T])
        m2_bias = sb("m2_bias", [P, T])
        y_image = sb("y_image", [P, 2 * HW])
        x_raw = sb("x_raw", [P, BLK])
        x_hi = sb("x_hi", [P, T, BLK], F32R)
        x_lo = sb("x_lo", [P, T, BLK], F32R)
        x_pad = sb("x_pad", [P, T, 2 * SEQ, PAD])
        u = sb("u", [P, T, 2 * SEQ, NH, L])
        xt_hi = sb("xt_hi", [P, 2, 2, P], F32R)
        xt_lo = sb("xt_lo", [P, 2, 2, P], F32R)
        score = sb("score", [QR, QW])
        expd = sb("expd", [QR, QW])
        row_max = sb("row_max", [QR, 8])
        row_sum = sb("row_sum", [QR, 8])
        row_rec = sb("row_rec", [QR, 8])
        prob = sb("prob", [QR, 8, PAD])
        pt_hi = sb("pt_hi", [P, 2, NH * L], F32R)
        pt_lo = sb("pt_lo", [P, 2, NH * L], F32R)
        z = sb("z", [P, T, NH, NH, 2 * SEQ, LQ])
        ax = sb("ax", [P, HW])
        ay = sb("ay", [P, 2 * HW])
        x_tail = sb("x_tail", [P, T, BLK])
        cpin_hi = sb("cpin_hi", [P, T, BLK], F32R)
        cpin_lo = sb("cpin_lo", [P, T, BLK], F32R)
        net = sb("net", [P, T, BLK])
        net_hi = sb("net_hi", [P, T, BLK], F32R)
        net_lo = sb("net_lo", [P, T, BLK], F32R)
        hid = sb("hid", [P, FT, BLK])
        hid_hi = sb("hid_hi", [P, FT, BLK], F32R)
        hid_lo = sb("hid_lo", [P, FT, BLK], F32R)

        y_spare = y_image[:, 0:2 * T * BLK].rearrange("p (a t n) -> p a t n", a=2, t=T)
        nets = [net[:, :, :], y_spare[:, 0]]
        cpins = [hid[:, 0:T, :], y_spare[:, 1]]

        stage = ay[:, 0:T * 4 * NH * P].rearrange("p (b w h c) -> p b w h c", b=T, w=4, h=NH)
        st_q, st_k, st_v, st_p = (stage[:, :, w] for w in range(4))
        spare = ay[:, T * 4 * NH * P:T * 4 * NH * P + 3 * T * DIM]
        st_cp = spare[:, 0:T * DIM].rearrange("p (t o) -> p t o", t=T)
        st_m1 = spare[:, T * DIM:3 * T * DIM].rearrange("p (t o) -> p t o", t=T)
        st_m2 = hid[:, :, 0:DIM]

        ps_score = bank("ps_score")
        ps_pt = bank("ps_pt")
        ps_z = [bank("ps_z0"), bank("ps_z1")]
        ps_un = [bank("ps_un0"), bank("ps_un1")]
        ps_mlp = [bank("ps_mlp0"), bank("ps_mlp1")]

        ps_hid = [*ps_mlp, *ps_un]
        ps_cp = [ps_score, ps_pt]
        ps_out = ps_z
        ps_o = [ps_z[1], ps_mlp[1], ps_pt, ps_mlp[0]]

        vectors_in = sem("vectors_in")
        qk_in = [sem("qk_x_in"), sem("qk_y_in")]
        vp_in = sem("vp_in")
        rel_in = sem("rel_in")
        mlp_in = sem("mlp_in")
        pads_zeroed = sem("pads_zeroed")
        ident_made = sem("ident_made")
        u_prep = sem("u_prep")
        o_prep = sem("o_prep")
        uhi_prep = sem("uhi_prep")
        ulo_prep = sem("ulo_prep")
        obias_prep = sem("obias_prep")
        o_even_prep = sem("o_even_prep")
        o_odd_prep = sem("o_odd_prep")
        bias_prep = sem("bias_prep")
        mlp_scaled = sem("mlp_scaled")
        mlp_hi_prep = sem("mlp_hi_prep")
        mlp_lo_prep = sem("mlp_lo_prep")
        y_loaded = sem("y_loaded")
        x_loaded = sem("x_loaded")
        tail_loaded = sem("tail_loaded")
        stored = sem("stored")
        xhi_made = sem("xhi_made")
        xlo_made = sem("xlo_made")
        xpad_made = sem("xpad_made")
        xt_done = sem("xt_done")
        xthi_made = sem("xthi_made")
        xtlo_made = sem("xtlo_made")
        pt_done = sem("pt_done")
        pthi_made = sem("pthi_made")
        ptlo_made = sem("ptlo_made")
        s_done = sem("s_done")
        added = sem("added")
        maxed = sem("maxed")
        shifted = sem("shifted")
        exped = sem("exped")
        summed = sem("summed")
        inverted = sem("inverted")
        prob_made = sem("prob_made")
        z_done = sem("z_done")
        z0_out = sem("z0_out")
        z1_out = sem("z1_out")
        u_done = sem("u_done")
        u_out = sem("u_out")
        o_done = sem("o_done")
        o_out = sem("o_out")
        cpin_x_made = sem("cpin_x_made")
        cpin_y_made = sem("cpin_y_made")
        cpinhi_made = sem("cpinhi_made")
        cpinlo_x_made = sem("cpinlo_x_made")
        cpinlo_y_made = sem("cpinlo_y_made")
        cp_done = sem("cp_done")
        net_made = sem("net_made")
        nethi_made = sem("nethi_made")
        netlo_made = sem("netlo_made")
        m1_done = sem("m1_done")
        hid_made = sem("hid_made")
        hidhi_made = sem("hidhi_made")
        hidlo_a_made = sem("hidlo_a_made")
        hidlo_b_made = sem("hidlo_b_made")
        m2_done = sem("m2_done")
        out_made = sem("out_made")

        def chunk_of(ap, c, t0, nt):
            src = ap[bass.ds(c // STEPS_IMG, 1), t0 * P:(t0 + nt) * P, bass.ds((c % STEPS_IMG) * BLK, BLK)]
            return src.rearrange("b (t p) n -> p (b t) n", p=P)

        def y_block(buf, s):
            v = buf[:, :].rearrange("p (a h w) -> p a w h", a=2, h=L)
            img, q = s // STEPS_IMG, s % STEPS_IMG
            return v[:, bass.ds(img % 2, 1), bass.ds(q * 2 * SEQ, 2 * SEQ), :].rearrange("p a w h -> p (a w) h")

        block = ctx.enter_context(nc.Block())

        @block.sync
        def _(sp):
            def load_weights(b, ws, sem_in):
                for w in ws:
                    src = (wq, wk, wv, wpT)[w]
                    sp.dma_start(stage[:, b, w], src[b].rearrange("(h d) c -> d h c", d=P)).then_inc(sem_in, 16)

            def load_rel(b):
                for h in range(NH):
                    w = 2 * L - 1
                    src = rel_tiled[b, h, L - 1:L - 1 + L * (w - 1)].rearrange("(i j) -> i j", j=w - 1)[:, 0:L]
                    sp.dma_start(rel[L * (h % 2):L * (h % 2) + L, b, h // 2, :], src).then_inc(rel_in, 16)

            load_weights(0, (0, 1), qk_in[0])
            sp.dma_start(x_raw[:, :], chunk_of(x, 0, 0, 1)[:, 0, :]).then_inc(x_loaded, 16)
            load_weights(1, (0, 1), qk_in[1])
            load_rel(0)
            load_rel(1)
            sp.dma_start(y_image[:, 0:HW], x[0, P:2 * P, :]).then_inc(y_loaded, 16)
            load_weights(0, (2, 3), vp_in)
            load_weights(1, (2, 3), vp_in)
            sp.dma_start(st_cp, cpT.rearrange("(t p) o -> p t o", p=P)).then_inc(mlp_in, 16)
            sp.dma_start(st_m2, m2T.rearrange("(t p) o -> p t o", p=P)).then_inc(mlp_in, 16)
            sp.dma_start(st_m1, m1T.rearrange("(t p) o -> p t o", p=P)).then_inc(mlp_in, 16)
            for n in range(2):
                sp.dma_start(ls_bc[:, n, :], ls_rows[n:n + 1, :].to_broadcast([P, DIM])).then_inc(mlp_in, 16)

            def load_y(s):
                sp.wait_ge(xpad_made, 2 * s + 2)
                sp.wait_ge(xlo_made, 2 * s + 2)
                n = s + STEPS_IMG
                at = (n // STEPS_IMG) % 2 * HW + n % STEPS_IMG * BLK
                sp.dma_start(y_image[:, bass.ds(at, BLK)], chunk_of(x, n, 1, 1)[:, 0, :]).then_inc(y_loaded, 16)

            def load_x(s):
                sp.wait_ge(xpad_made, 2 * s - 1)
                sp.wait_ge(xlo_made, 2 * s - 1)
                sp.dma_start(x_raw[:, :], chunk_of(x, s, 0, 1)[:, 0, :]).then_inc(x_loaded, 16)

            def load_tail(c):
                sp.dma_start(x_tail[:, :, :], chunk_of(x, c, 0, T)).then_inc(tail_loaded, 16)

            def store(c, buf):
                sp.wait_ge(out_made, 2 * c + 4)
                sp.dma_start(chunk_of(out, c, 0, T), nets[buf]).then_inc(stored, 16)

            def step(s, y=False, xr=False, tail=False, out=False):
                c = s - STEPS_IMG
                if y:
                    load_y(s)
                if out:
                    store(c - 1, 0)
                if xr:
                    load_x(s + 2)
                if tail:
                    sp.wait_ge(net_made, 2 * c + 2)
                    load_tail(c + 1)

            def last_image(c, buf, more=True):
                if more:
                    sp.wait_ge(net_made, 2 * c + 4)
                    load_tail(c + 2)
                store(c, buf)

            load_x(1)
            with sp.Fori(0, STEPS_IMG) as s:
                step(s, y=True, xr=True)
            load_tail(0)
            step(STEPS_IMG, y=True, xr=True, tail=True)
            with sp.Fori(STEPS_IMG + 1, STEPS - STEPS_IMG) as s:
                step(s, y=True, xr=True, tail=True, out=True)
            with sp.Fori(STEPS - STEPS_IMG, STEPS - 2) as s:
                step(s, xr=True, tail=True, out=True)
            for s in range(STEPS - 2, STEPS):
                step(s, tail=True, out=True)
            last_image(LAST - 1, 0)
            with sp.Fori(LAST, STEPS - 3, 2) as c:
                last_image(c, 1)
                last_image(c + 1, 0)
            last_image(STEPS - 3, 1)
            last_image(STEPS - 2, 0, more=False)
            last_image(STEPS - 1, 1, more=False)
            sp.wait_ge(stored, 16 * (STEPS + 1))

        @block.tensor
        def _(pe):
            mm = nc.tensor.matmul

            pe.wait_ge(vectors_in, 16)
            for b in range(T):
                pe.wait_ge(qk_in[b], 32)
                for h in range(NH):
                    mm(ps_un[b][:, h * P:(h + 1) * P], st_q[:, b, h], st_k[:, b, h], start=True, stop=True)
                for h in range(NH):
                    n = b * NH + h
                    last = mm(ps_mlp[b][:, h:h + 1], st_k[:, b, h], cols[:, C_QB + n:C_QB + n + 1],
                              start=True, stop=True)
                last.then_inc(u_prep, 1)

            def output_weights():
                pe.wait_ge(vp_in, 64)
                for b in range(T):
                    for m in range(NH):
                        last = mm(ps_mlp[0][:, b * NH:(b + 1) * NH], st_p[:, b, m],
                                  cols[:, C_VB + b * NH:C_VB + (b + 1) * NH], start=(m == 0), stop=(m == NH - 1))
                last.then_inc(o_prep, 1)
                for b in range(T):
                    for h in range(NH):
                        if h == NH - 1 and b == 0:
                            pe.wait_ge(obias_prep, T)
                        if b:
                            pe.wait_ge(o_odd_prep if h % 2 else o_even_prep, h // 2 + 1)
                        mm(ps_o[h][:, :], st_v[:, b, h], st_p[:, b].rearrange("p m o -> p (m o)"),
                           start=True, stop=True).then_inc(o_prep, 1)

            pe.sem_inc(s_done, 2)
            pe.sem_inc(z_done, 1)
            pe.sem_inc(o_done, 3)
            pe.sem_inc(cp_done, 2)
            pe.sem_inc(m1_done, 4)
            pe.sem_inc(m2_done, 2)

            def three(ps, w_hi, w_lo, a_hi, a_lo, first, last):
                mm(ps, w_lo, a_hi, start=first, stop=False)
                mm(ps, w_hi, a_lo, start=False, stop=False)
                return mm(ps, w_hi, a_hi, start=False, stop=last)

            def values_t(g, k):
                br, kk = k // 2, k % 2
                pe.wait_ge(xpad_made, g // 2 + 1 if isinstance(g, int) else 2 * ((g - k) // 4) + br + 1)
                if not isinstance(g, int) or g:
                    pe.wait_ge(z0_out, g)
                    pe.wait_ge(xtlo_made, g)
                for pair in range(2):
                    last = nc.tensor.transpose(ps_z[0][:, pair * P:(pair + 1) * P],
                                               x_pad[:, br, 4 * kk + 2 * pair:4 * kk + 2 * pair + 2, :]
                                               .rearrange("p s i -> p (s i)"), ident[:, :])
                last.then_inc(xt_done, 1)

            def scores(g, blk, k):
                br, kk = k // 2, k % 2
                pe.wait_ge(u_out, 4 * blk + 4)
                if not isinstance(g, int) or g:
                    pe.wait_ge(added, g)
                for pair in range(2):
                    for hp in range(2):
                        for sq in range(2):
                            n = 4 * kk + 2 * pair + sq
                            at = ((hp * 2 + pair) * 2 + sq) * L
                            last = mm(ps_score[0:QR, at:at + L],
                                      u[:, br, n, 2 * hp:2 * hp + 2, :].rearrange("p h i -> p (h i)"),
                                      x_pad[:, br, n, 0:L], start=True, stop=True)
                last.then_inc(s_done, 1)

            def probs_t(g):
                pe.wait_ge(prob_made, g + 1)
                pe.wait_ge(pthi_made, g + 1)
                pe.wait_ge(ptlo_made, g + 1)
                for n in range(4):
                    pair, hp = n // 2, n % 2
                    rows = slice(4 * hp + 2 * pair, 4 * hp + 2 * pair + 2)
                    last = nc.tensor.transpose(ps_pt[:, n * QR:(n + 1) * QR],
                                               prob[:, rows, :].rearrange("p s j -> p (s j)"),
                                               ident[0:QR, 0:QR])
                last.then_inc(pt_done, 1)

            def weigh(g, k, more):
                pe.wait_ge(pthi_made, g + 2)
                pe.wait_ge(ptlo_made, g + 2)
                pe.wait_ge(xthi_made, g + 1)
                pe.wait_ge(xtlo_made, g + 2 if more else g + 1)
                pe.wait_ge(z1_out, g + 1)
                pe.wait_ge(z0_out, g + 1)
                for pair in range(2):
                    for n, (x_part, p_part) in enumerate(((xt_lo, pt_hi), (xt_hi, pt_lo), (xt_hi, pt_hi))):
                        for sq in range(2):
                            rows = slice(PAD * sq, PAD * sq + L)
                            last = mm(ps_z[sq][:, pair * NH * L:(pair + 1) * NH * L], x_part[rows, k % 2, pair, :],
                                      p_part[rows, pair, :], start=(n == 0), stop=(n == 2))
                last.then_inc(z_done, 1)

            def queries(blk, br, h, bk, free):
                pe.wait_ge(xhi_made, blk + 1)
                pe.wait_ge(xlo_made, blk + 1)
                if free is not None:
                    pe.wait_ge(*free)
                three(ps_un[bk][:, 0:BLK], u_hi[:, br, h], u_lo[:, br, h], x_hi[:, br, :], x_lo[:, br, :],
                      True, True).then_inc(u_done, 1)

            def project(g, br, half, bk):
                quads = min(g, 4 * STEPS) if isinstance(g, int) else g
                pe.wait_ge(z0_out, quads + 1)
                pe.wait_ge(z1_out, quads + 1)
                if isinstance(g, int) and g > 4 * STEPS - 4:
                    pe.wait_ge(u_out, 2 * NH * STEPS)
                    pe.wait_ge(o_out, g)
                else:
                    pe.wait_ge(u_out, 2 * g + 5)
                n = BLK // NH
                for h in range(2):
                    for m in range(NH):
                        last = mm(ps_un[bk][:, h * n:(h + 1) * n], o_w[:, br, 2 * half + h, m],
                                  z[:, br, 2 * half + h, m].rearrange("p s i -> p (s i)"),
                                  start=(m == 0), stop=(m == NH - 1))
                last.then_inc(o_done, 1)

            def compress(c):
                for t in range(T):
                    pe.wait_ge(out_made, 2 * c + 1 + t)
                for i in range(T):
                    pe.wait_ge(cpinhi_made, 2 * c + 3 + i)
                    pe.wait_ge((cpinlo_x_made, cpinlo_y_made)[i], c + 1)
                    for t in range(T):
                        last = compress_part(ps_mlp[t], t, i)
                        if i == T - 1:
                            last.then_inc(cp_done, 1)

            def compress_part(bank, t, i):
                return three(bank[:, 0:BLK], cp_hi[:, i, t * P:(t + 1) * P], cp_lo[:, i, t * P:(t + 1) * P],
                             cpin_hi[:, i, :], cpin_lo[:, i, :], i == 0, i == T - 1)

            def expand(c, t):
                pe.wait_ge(nethi_made, c + 1)
                pe.wait_ge(netlo_made, c + 1)
                if t >= 2:
                    pe.wait_ge(hid_made, 4 * c + t - 1)
                else:
                    pe.wait_ge(net_made, 2 * c + 1 + t)
                expand_tile(ps_mlp[t % 2], t)

            def expand_tile(bank, t):
                for i in range(T):
                    last = three(bank[:, 0:BLK], m1_hi[:, i, t * P:(t + 1) * P], m1_lo[:, i, t * P:(t + 1) * P],
                                 net_hi[:, i, :], net_lo[:, i, :], i == 0, i == T - 1)
                last.then_inc(m1_done, 1)

            def contract(c, t):
                pe.wait_ge(hid_made, 4 * c + 3 + t)
                contract_tile(c, ps_mlp[t], t)

            def contract_tile(c, bank, t):
                for i in range(FT):
                    if t == 0 and i % 2 == 0:
                        pe.wait_ge(hidhi_made, 2 * c + 3 + i // 2)
                        pe.wait_ge(hidlo_a_made if i == 0 else hidlo_b_made, c + 2)
                    last = three(bank[:, 0:BLK], m2_hi[:, i, t * P:(t + 1) * P], m2_lo[:, i, t * P:(t + 1) * P],
                                 hid_hi[:, i, :], hid_lo[:, i, :], i == 0, i == FT - 1)
                last.then_inc(m2_done, 1)

            def step(s, tail=False, out=False, first=False, last=False):
                c = s - STEPS_IMG
                for k in range(4):
                    g = 4 * s + k
                    more = not (last and k == 3)
                    if more:
                        values_t(g + 1, (k + 1) % 4)
                    probs_t(g)
                    if more:
                        scores(g + 1, 2 * s + (k + 1) // 2, (k + 1) % 4)
                    if not (first and k < 2):
                        project(g, 0 if k >= 2 else 1, k % 2, k % 2)
                    weigh(g, k, more)
                    if not (last and k > 0):
                        br = (k + 3) // 2 % 2
                        queries(2 * s + (k + 3) // 2, br, 2 * ((k + 3) % 2), 1 - k % 2, (u_out, 2 * g + 6))
                        queries(2 * s + (k + 3) // 2, br, 2 * ((k + 3) % 2) + 1, k % 2, (o_out, g + 2))
                    if out and k == 0:
                        contract(c - 1, 0)
                        contract(c - 1, 1)
                    if tail and k == 1:
                        compress(c)
                    if tail and k >= 2:
                        expand(c, 2 * k - 4)
                        expand(c, 2 * k - 3)

            def first_queries(m):
                queries(m // 4, m // 4, m % 4, m % 2, (u_out, m - 1) if m >= 2 else None)

            for m in range(NH):
                if m < T:
                    pe.wait_ge(uhi_prep, m + 1)
                    pe.wait_ge(ulo_prep, 2 * m + 1)
                first_queries(m)
            pe.wait_ge(ident_made, 2)
            pe.wait_ge(pads_zeroed, 2)
            values_t(0, 0)
            scores(0, 0, 0)
            output_weights()
            first_queries(NH)
            first_queries(NH + 1)
            pe.wait_ge(o_even_prep, 2 * T)
            pe.wait_ge(o_odd_prep, 2 * T)
            step(0, first=True)
            with pe.Fori(1, STEPS_IMG) as s:
                step(s)
            pe.wait_ge(mlp_hi_prep, 3)
            pe.wait_ge(mlp_lo_prep, 3)
            step(STEPS_IMG, tail=True)
            with pe.Fori(STEPS_IMG + 1, STEPS - 1) as s:
                step(s, tail=True, out=True)
            step(STEPS - 1, tail=True, out=True, last=True)
            project(4 * STEPS, 1, 0, 0)
            project(4 * STEPS + 1, 1, 1, 1)

            def last_compress(c):
                pe.wait_ge(net_made, 2 * c)
                for i in range(T):
                    pe.wait_ge(cpinhi_made, 2 * c + 3 + i)
                    pe.wait_ge((cpinlo_x_made, cpinlo_y_made)[i], c + 1)
                for t in range(T):
                    for i in range(T):
                        last = compress_part(ps_cp[t], t, i)
                    last.then_inc(cp_done, 1)

            def last_image(c, more=True):
                pe.wait_ge(nethi_made, c + 1)
                pe.wait_ge(netlo_made, c + 1)
                for t in range(FT):
                    if isinstance(c, int) and c == LAST:
                        pe.wait_ge(*((out_made, 2 * c + 1 + t) if t < 2 else (o_out, 4 * STEPS + 3)))
                    else:
                        pe.wait_ge(hid_made, 4 * c - 3 + t)
                    expand_tile(ps_hid[t], t)
                if more:
                    last_compress(c + 1)
                for t in range(T):
                    pe.wait_ge(out_made, 2 * c + 1 + t)
                    contract_tile(c, ps_out[t], t)

            contract(LAST - 1, 0)
            pe.wait_ge(added, 4 * STEPS)
            last_compress(LAST)
            contract(LAST - 1, 1)
            last_image(LAST)
            with pe.Fori(LAST + 1, STEPS - 1) as c:
                last_image(c)
            last_image(STEPS - 1, more=False)

        @block.scalar
        def _(act):
            act.dma_start(cols[:, :], columns).then_inc(vectors_in, 16)
            for b in range(T):
                act.wait_ge(u_prep, b + 1)
                nc.scalar.activation(u_hi[:, b].rearrange("p h c -> p (h c)"), ps_un[b][:, :], ACT.Copy,
                                     scale=SCALE).then_inc(uhi_prep, 1)
            act.sem_inc(pthi_made, 1)
            act.sem_inc(cpinhi_made, 2)
            act.sem_inc(z1_out, 1)

            def query_out(m, blk, h, br, bk):
                act.wait_ge(u_done, m + 1)
                if not isinstance(m, int) or blk:
                    act.wait_ge(s_done, 2 * blk)
                nc.scalar.activation(u[:, br, :, h, :], ps_un[bk][:, 0:BLK].rearrange("p (s i) -> p s i", i=L),
                                     ACT.Identity, bias=u_bias[:, br, h:h + 1]).then_inc(u_out, 1)

            def exps(g):
                act.wait_ge(shifted, g + 1)
                if not isinstance(g, int) or g:
                    act.wait_ge(prob_made, g)
                nc.scalar.activation(expd[:, :], score[:, :], ACT.Exp).then_inc(exped, 1)

            def z_out(g, k):
                act.wait_ge(z_done, g + 2)
                if k % 2 == 0:
                    act.wait_ge(o_done, g + 1)
                for sq, made in ((0, z0_out), (1, z1_out)):
                    src = ps_z[sq][:, 0:2 * NH * L].rearrange("p (a n i) -> p a n i", a=2, i=LQ)
                    dst = z[:, k // 2].rearrange("p h m (q a s) i -> p q s a (h m) i", q=2, a=2)[:, k % 2, sq]
                    nc.scalar.activation(dst, src, ACT.Copy).then_inc(made, 1)

            def step(s, tail=False, last=False):
                c = s - STEPS_IMG
                for k in range(4):
                    g = 4 * s + k
                    act.wait_ge(pt_done, g + 1)
                    act.wait_ge(z_done, g + 1)
                    nc.scalar.activation(pt_hi[:, :, :].rearrange("p a (h m i) -> p (a h) m i", m=NH, i=LQ),
                                         ps_pt[:, 0:QW].rearrange("p (n i m) -> p n m i", i=LQ, m=NH),
                                         ACT.Copy).then_inc(pthi_made, 1)
                    if tail and k == 1:
                        split_cpin(c, 0)
                    if tail and k == 2:
                        split_net(c, 0)
                    if not (last and k == 3):
                        exps(g + 1)
                    if tail and k == 1:
                        split_cpin(c, 1)
                    z_out(g, k)
                    if not (last and k > 0):
                        for hh in range(2):
                            query_out(2 * g + 6 + hh, 2 * s + (k + 3) // 2, 2 * ((k + 3) % 2) + hh,
                                      (k + 3) // 2 % 2, (k + 1 + hh) % 2)
                    if tail and k >= 2:
                        hidden(c, 2 * k - 4)
                        hidden(c, 2 * k - 3)

            def split_cpin(c, t, buf=0):
                act.wait_ge((cpin_x_made, cpin_y_made)[t], c + 1)
                act.wait_ge(cp_done, 2 * c + 2)
                nc.scalar.activation(cpin_hi[:, t, :], cpins[buf][:, t, :], ACT.Copy).then_inc(cpinhi_made, 1)

            def split_net(c, buf):
                act.wait_ge(net_made, 2 * c + 2)
                act.wait_ge(m1_done, 4 * c + 4)
                nc.scalar.activation(net_hi[:, :, :].rearrange("p t n -> p (t n)"),
                                     nets[buf].rearrange("p t n -> p (t n)"), ACT.Copy).then_inc(nethi_made, 1)

            def hidden(c, t, bank=None):
                if t == 0:
                    act.wait_ge(hidhi_made, 2 * c + 2)
                    act.wait_ge(hidlo_a_made, c + 1)
                    act.wait_ge(hidlo_b_made, c + 1)
                act.wait_ge(m1_done, 4 * c + t + 5)
                nc.scalar.activation(hid[:, t, :], (bank or ps_mlp[t % 2])[:, 0:BLK], ACT.Gelu,
                                     bias=cols[:, C_M1B + t:C_M1B + t + 1]).then_inc(hid_made, 1)

            act.wait_ge(ulo_prep, 2 * T)
            act.wait_ge(pads_zeroed, 2)
            for m in range(NH):
                query_out(m, 0, m, 0, m % 2)
            exps(0)
            for b in range(T):
                for h in (1, 3):
                    act.wait_ge(o_prep, 2 + NH * b + h)
                    nc.scalar.activation(o_w[:, b, h].rearrange("p m o -> p (m o)"), ps_o[h][:, :],
                                         ACT.Copy).then_inc(o_odd_prep, 1)
            for m in (NH, NH + 1):
                query_out(m, 1, m % NH, 1, m % 2)
            act.wait_ge(bias_prep, 2)
            with act.Fori(0, STEPS_IMG) as s:
                step(s)
            with act.Fori(STEPS_IMG, STEPS - 1) as s:
                step(s, tail=True)
            step(STEPS - 1, tail=True, last=True)

            def last_image(c, buf, more=True):
                hidden(c, 0, ps_hid[0])
                if more:
                    split_cpin(c + 1, 0, 1)
                    split_cpin(c + 1, 1, 1)
                for t in range(1, FT):
                    hidden(c, t, ps_hid[t])
                if more:
                    split_net(c + 1, 1 - buf)

            split_cpin(LAST, 0, 1)
            split_cpin(LAST, 1, 1)
            split_net(LAST, 1)
            with act.Fori(LAST, STEPS - 1, 2) as c:
                last_image(c, 1)
                last_image(c + 1, 0)
            last_image(STEPS - 1, 1, more=False)

        @block.vector
        def _(dve):
            nc.vector.memset(x_pad[:, :, :, L:PAD], 0.0).then_inc(pads_zeroed, 1)
            nc.vector.memset(prob[:, :, L:PAD], 0.0).then_inc(pads_zeroed, 1)

            dve.sem_inc(z0_out, 1)
            dve.sem_inc(o_out, 3)
            dve.sem_inc(hidhi_made, 2)
            dve.sem_inc(hidlo_a_made, 1)
            dve.sem_inc(out_made, 2)
            dve.sem_inc(ptlo_made, 1)
            dve.sem_inc(stored, 16)

            def split_hi(blk, s, br):
                if br == 0:
                    dve.wait_ge(x_loaded, 16 * s + 16)
                    src = x_raw[:, :].rearrange("p (s i) -> p s i", i=L)
                else:
                    dve.wait_ge(y_loaded, 16 * (STEPS_IMG * (s // STEPS_IMG) + 1))
                    src = y_block(y_image, s)
                if not isinstance(blk, int) or blk >= 2:
                    dve.wait_ge(u_done, 4 * blk - 4)
                nc.vector.tensor_scalar(x_hi[:, br, :].rearrange("p (s i) -> p s i", i=L), src, 1.0, None,
                                        ALU.mult).then_inc(xhi_made, 1)

            def pad(blk, s, br):
                src = x_raw[:, :].rearrange("p (s i) -> p s i", i=L) if br == 0 else y_block(y_image, s)
                if not isinstance(blk, int) or blk >= 2:
                    dve.wait_ge(s_done, 2 * blk)
                    dve.wait_ge(xt_done, 2 * blk - 2)
                nc.vector.tensor_scalar(x_pad[:, br, :, 0:L], src, 1.0, None, ALU.mult).then_inc(xpad_made, 1)

            def softmax_a(g, k, between=None):
                br = k // 2
                dve.wait_ge(s_done, g + 3)
                if not isinstance(g, int) or g:
                    dve.wait_ge(exped, g)
                nc.vector.tensor_tensor(score[:, :].rearrange("p (h n j) -> p h n j", h=2, j=L),
                                        ps_score[0:QR, 0:QW].rearrange("p (h n j) -> p h n j", h=2, j=L),
                                        rel[:, br].unsqueeze(2).to_broadcast([QR, 2, SEQ, L]),
                                        ALU.add).then_inc(added, 1)
                if between:
                    between()
                rows = score[:, :].rearrange("p (n j) -> p n j", j=L)
                dve.wait_ge(added, g + 1)
                nc.vector.tensor_reduce(row_max[:, :], rows, AX_X, ALU.max).then_inc(maxed, 1)
                dve.wait_ge(maxed, g + 1)
                nc.vector.tensor_tensor(rows, rows, row_max[:, :].unsqueeze(2).to_broadcast([QR, 8, L]),
                                        ALU.subtract).then_inc(shifted, 1)

            def softmax_b(g, between=None):
                dve.wait_ge(exped, g + 1)
                nc.vector.tensor_reduce(row_sum[:, :], expd[:, :].rearrange("p (n j) -> p n j", j=L), AX_X,
                                        ALU.add).then_inc(summed, 1)
                dve.wait_ge(summed, g + 1)
                if not isinstance(g, int) or g:
                    dve.wait_ge(prob_made, g)
                nc.vector.reciprocal(row_rec[:, :], row_sum[:, :]).then_inc(inverted, 1)
                if between:
                    between()

            def values_out(g, k):
                dve.wait_ge(xt_done, g + 1)
                if not isinstance(g, int) or g:
                    dve.wait_ge(z_done, g)
                nc.vector.tensor_copy(xt_hi[:, k % 2].rearrange("p a c -> p (a c)"),
                                      ps_z[0][:, 0:2 * P]).then_inc(xthi_made, 1)
                dve.wait_ge(xthi_made, g + 1)
                nc.vector.tensor_tensor(xt_lo[:, k % 2].rearrange("p a c -> p (a c)"), ps_z[0][:, 0:2 * P],
                                        xt_hi[:, k % 2].rearrange("p a c -> p (a c)").bitcast(F32),
                                        ALU.subtract).then_inc(xtlo_made, 1)

            def probs_lo(g):
                dve.wait_ge(pthi_made, g + 2)
                dve.wait_ge(z_done, g + 1)
                nc.vector.tensor_tensor(pt_lo[:, :, :].rearrange("p a (h m i) -> p (a h) m i", m=NH, i=LQ),
                                        ps_pt[:, 0:QW].rearrange("p (n i m) -> p n m i", i=LQ, m=NH),
                                        pt_hi[:, :, :].rearrange("p a (h m i) -> p (a h) m i", m=NH, i=LQ)
                                        .bitcast(F32), ALU.subtract).then_inc(ptlo_made, 1)

            def attention_out(g, s, br, half, tail):
                dve.wait_ge(o_done, g + 2)
                src = ps_un[half][:, 0:BLK // 2].rearrange("p (n s i) -> p n s i", n=2, i=LQ)
                if br == 0:
                    if tail:
                        dve.wait_ge(cpin_x_made, s - STEPS_IMG + 1)
                    dst = ax[:, bass.ds(s % STEPS_IMG * BLK, BLK)].rearrange("p (s n i) -> p n s i", n=NH, i=LQ)
                else:
                    dst = y_block(ay, s).rearrange("p s (n i) -> p n s i", n=NH)
                heads = slice(2 * half, 2 * half + 2)
                bias = o_bias[:, br, heads].unsqueeze(2).unsqueeze(3).to_broadcast([P, 2, 2 * SEQ, LQ])
                nc.vector.tensor_tensor(dst[:, heads], src, bias, ALU.add).then_inc(o_out, 1)

            def normalise(g):
                dve.wait_ge(inverted, g + 1)
                if not isinstance(g, int) or g:
                    dve.wait_ge(pt_done, g)
                nc.vector.tensor_tensor(prob[:, :, 0:L], expd[:, :].rearrange("p (n j) -> p n j", j=L),
                                        row_rec[:, :].unsqueeze(2).to_broadcast([QR, 8, L]),
                                        ALU.mult).then_inc(prob_made, 1)

            def step(s, tail=False, out=False, first=False, last=False):
                c = s - STEPS_IMG
                for k in range(4):
                    g = 4 * s + k
                    more = not (last and k == 3)
                    if more:
                        values_out(g + 1, (k + 1) % 4)
                    probs_lo(g)
                    if out and k == 0:
                        split_hidden_hi(c - 1, 2)
                    if tail and k == 3:
                        split_hidden_hi(c, 0)

                    def projected():
                        if k >= 2:
                            attention_out(g, s, 0, k - 2, tail)
                        elif not first:
                            attention_out(g, s - 1, 1, k, tail)

                    early = out and k == 0
                    if more:
                        softmax_a(g + 1, (k + 1) % 4, projected if early else None)
                    if not early:
                        projected()
                    if tail and k == 1:
                        add_input_y(c)
                    if more:
                        softmax_b(g + 1, (lambda: split_cpin_y(c)) if tail and k == 1 else None)
                        normalise(g + 1)
                    if not last:
                        if k % 2 == 0:
                            split_hi(2 * s + 2 + k // 2, s + 1, k // 2)
                        else:
                            pad(2 * s + 2 + k // 2, s + 1, k // 2)
                    if out and k == 0:
                        add_out(c - 1, 0)
                    if tail and k == 1:
                        add_net(c, 0, 16 * c + 16)
                    if tail and k == 3:
                        split_hidden_lo(c)

            def add_input_y(c, buf=0):
                dve.wait_ge(o_out, 4 * (STEPS_IMG * (c // STEPS_IMG) + STEPS_IMG) + 3)
                dve.wait_ge(cpinhi_made, 2 * c + 2)
                dve.wait_ge(tail_loaded, 16 * c + 16)
                at = c % STEPS_IMG * BLK + c // STEPS_IMG % 2 * HW
                nc.vector.tensor_tensor(cpins[buf][:, 1, :], ay[:, bass.ds(at, BLK)], x_tail[:, 1, :],
                                        ALU.add).then_inc(cpin_y_made, 1)

            def split_cpin_y(c, buf=0):
                dve.wait_ge(cp_done, 2 * c + 2)
                dve.wait_ge(cpinhi_made, 2 * c + 4)
                nc.vector.tensor_tensor(cpin_lo[:, 1, :], cpins[buf][:, 1, :], cpin_hi[:, 1, :].bitcast(F32),
                                        ALU.subtract).then_inc(cpinlo_y_made, 1)

            def add_net(c, buf, free, banks=ps_mlp):
                for t in range(T):
                    dve.wait_ge(cp_done, 2 * c + t + 3)
                    dve.wait_ge(stored, free)
                    dve.wait_ge(tail_loaded, 16 * c + 16)
                    nc.vector.scalar_tensor_tensor(out=nets[buf][:, t, :], in0=banks[t][:, 0:BLK],
                                                   scalar=cp_bias[:, t:t + 1], in1=x_tail[:, t, :],
                                                   op0=ALU.add, op1=ALU.add).then_inc(net_made, 1)

            def split_hidden_hi(c, t):
                dve.wait_ge(m2_done, 2 * c + 2)
                dve.wait_ge(hid_made, 4 * c + t + 2)
                nc.vector.tensor_copy(hid_hi[:, t:t + 2, :].rearrange("p t n -> p (t n)"),
                                      hid[:, t:t + 2, :].rearrange("p t n -> p (t n)")).then_inc(hidhi_made, 1)

            def split_hidden_lo(c):
                dve.wait_ge(hidhi_made, 2 * c + 3)
                nc.vector.tensor_tensor(hid_lo[:, 0:2, :].rearrange("p t n -> p (t n)"),
                                        hid[:, 0:2, :].rearrange("p t n -> p (t n)"),
                                        hid_hi[:, 0:2, :].rearrange("p t n -> p (t n)").bitcast(F32),
                                        ALU.subtract).then_inc(hidlo_a_made, 1)

            def add_out(c, buf, banks=ps_mlp, tiles=range(T)):
                for t in tiles:
                    dve.wait_ge(m2_done, 2 * c + t + 3)
                    nc.vector.scalar_tensor_tensor(out=nets[buf][:, t, :], in0=banks[t][:, 0:BLK],
                                                   scalar=m2_bias[:, t:t + 1], in1=nets[buf][:, t, :],
                                                   op0=ALU.add, op1=ALU.add).then_inc(out_made, 1)

            def output_weights_out(b, h):
                dve.wait_ge(o_prep, 2 + NH * b + h)
                nc.vector.tensor_copy(o_w[:, b, h].rearrange("p m o -> p (m o)"),
                                      ps_o[h][:, :]).then_inc(o_even_prep, 1)

            split_hi(0, 0, 0)
            pad(0, 0, 0)
            for b in range(T):
                dve.wait_ge(u_prep, b + 1)
                dve.wait_ge(uhi_prep, b + 1)
                nc.vector.scalar_tensor_tensor(out=u_lo[:, b].rearrange("p h c -> p (h c)"), in0=ps_un[b][:, :],
                                               scalar=SCALE, in1=u_hi[:, b].rearrange("p h c -> p (h c)").bitcast(F32),
                                               op0=ALU.mult, op1=ALU.subtract).then_inc(ulo_prep, 1)
                nc.vector.tensor_scalar(u_bias[:, b, :], ps_mlp[b][:, 0:NH], SCALE, None,
                                        ALU.mult).then_inc(ulo_prep, 1)
            dve.wait_ge(vectors_in, 16)
            nc.vector.tensor_tensor(cp_bias[:, :], cols[:, C_CPB:C_CPB + T], cols[:, C_LS1:C_LS1 + T],
                                    ALU.mult).then_inc(bias_prep, 1)
            nc.vector.tensor_tensor(m2_bias[:, :], cols[:, C_M2B:C_M2B + T], cols[:, C_LS2:C_LS2 + T],
                                    ALU.mult).then_inc(bias_prep, 1)
            values_out(0, 0)
            dve.wait_ge(rel_in, 16 * T * NH)
            softmax_a(0, 0)
            dve.wait_ge(o_prep, 1)
            for b in range(T):
                nc.vector.tensor_scalar(o_bias[:, b, :], ps_mlp[0][:, b * NH:(b + 1) * NH],
                                        cols[:, C_PB + b:C_PB + b + 1], None, ALU.add).then_inc(obias_prep, 1)
            output_weights_out(0, 0)
            softmax_b(0)
            normalise(0)
            split_hi(1, 0, 1)
            pad(1, 0, 1)
            output_weights_out(0, 2)
            output_weights_out(1, 0)
            output_weights_out(1, 2)
            dve.wait_ge(obias_prep, T)
            dve.wait_ge(bias_prep, 2)
            step(0, first=True)
            with dve.Fori(1, STEPS_IMG) as s:
                step(s)
            step(STEPS_IMG, tail=True)
            with dve.Fori(STEPS_IMG + 1, STEPS - 1) as s:
                step(s, tail=True, out=True)
            step(STEPS - 1, tail=True, out=True, last=True)

            def last_image(c, buf, more=True):
                if more:
                    add_input_y(c + 1, 1)
                    split_cpin_y(c + 1, 1)
                split_hidden_hi(c, 0)
                split_hidden_lo(c)
                split_hidden_hi(c, 2)
                if more:
                    add_net(c + 1, 1 - buf, 16 * c + 16, ps_cp)
                add_out(c, buf, ps_out)

            split_hidden_hi(LAST - 1, 2)
            attention_out(4 * STEPS, STEPS - 1, 1, 0, True)
            attention_out(4 * STEPS + 1, STEPS - 1, 1, 1, True)
            add_input_y(LAST, 1)
            split_cpin_y(LAST, 1)
            add_out(LAST - 1, 0, tiles=(0,))
            add_net(LAST, 1, 16 * LAST, ps_cp)
            add_out(LAST - 1, 0, tiles=(1,))
            with dve.Fori(LAST, STEPS - 1, 2) as c:
                last_image(c, 1)
                last_image(c + 1, 0)
            last_image(STEPS - 1, 1, more=False)

        @block.gpsimd
        def _(pool):
            nc.gpsimd.memset(ident[:, :], 0.0).then_inc(ident_made, 1)
            pool.wait_ge(ident_made, 1)
            nc.gpsimd.affine_select(out=ident[:, :], in_=ident[:, :], compare_op=ALU.not_equal, fill=1.0, base=0,
                                    pattern=[[-1, P]], channel_multiplier=1).then_inc(ident_made, 1)

            def scale_mlp():
                pool.wait_ge(mlp_in, 16 * 5)
                for n, w in enumerate((st_cp, st_m2)):
                    tiles = w.shape[1]
                    nc.gpsimd.tensor_tensor(w, w, ls_bc[:, n, :].unsqueeze(1).to_broadcast([P, tiles, DIM]),
                                            ALU.mult).then_inc(mlp_scaled, 1)

            def split_mlp():
                pool.wait_ge(mlp_scaled, 2)
                parts = ((st_cp, cp_hi, cp_lo), (st_m1, m1_hi, m1_lo), (st_m2, m2_hi, m2_lo))
                for w, hi, lo in parts:
                    nc.gpsimd.tensor_copy(hi[:, :, :], w).then_inc(mlp_hi_prep, 1)
                for n, (w, hi, lo) in enumerate(parts):
                    pool.wait_ge(mlp_hi_prep, n + 1)
                    nc.gpsimd.tensor_tensor(lo[:, :, :], w, hi[:, :, :].bitcast(F32),
                                            ALU.subtract).then_inc(mlp_lo_prep, 1)

            def split_lo(blk, s, br):
                pool.wait_ge(xhi_made, blk + 1)
                pool.wait_ge(ident_made, 2)
                src = x_raw[:, :].rearrange("p (s i) -> p s i", i=L) if br == 0 else y_block(y_image, s)
                nc.gpsimd.tensor_tensor(x_lo[:, br, :].rearrange("p (s i) -> p s i", i=L), src,
                                        x_hi[:, br, :].rearrange("p (s i) -> p s i", i=L).bitcast(F32),
                                        ALU.subtract).then_inc(xlo_made, 1)

            def add_input_x(c, buf=0):
                if buf == 0:
                    pool.wait_ge(hidlo_a_made, c + 1)
                pool.wait_ge(o_out, 4 * (STEPS_IMG * (c // STEPS_IMG) + STEPS_IMG) + 1)
                pool.wait_ge(tail_loaded, 16 * c + 16)
                pool.wait_ge(ident_made, 2)
                nc.gpsimd.tensor_tensor(cpins[buf][:, 0, :], ax[:, bass.ds(c % STEPS_IMG * BLK, BLK)], x_tail[:, 0, :],
                                        ALU.add).then_inc(cpin_x_made, 1)

            def split_cpin_x(c, buf=0):
                pool.wait_ge(cp_done, 2 * c + 2)
                pool.wait_ge(cpinhi_made, 2 * c + 3)
                nc.gpsimd.tensor_tensor(cpin_lo[:, 0, :], cpins[buf][:, 0, :], cpin_hi[:, 0, :].bitcast(F32),
                                        ALU.subtract).then_inc(cpinlo_x_made, 1)

            def split_net(c, buf):
                pool.wait_ge(nethi_made, c + 1)
                pool.wait_ge(m1_done, 4 * c + 4)
                nc.gpsimd.tensor_tensor(net_lo[:, :, :].rearrange("p t n -> p (t n)"),
                                        nets[buf].rearrange("p t n -> p (t n)"),
                                        net_hi[:, :, :].rearrange("p t n -> p (t n)").bitcast(F32),
                                        ALU.subtract).then_inc(netlo_made, 1)

            def split_hidden(c):
                pool.wait_ge(hidhi_made, 2 * c + 4)
                nc.gpsimd.tensor_tensor(hid_lo[:, 2:4, :].rearrange("p t n -> p (t n)"),
                                        hid[:, 2:4, :].rearrange("p t n -> p (t n)"),
                                        hid_hi[:, 2:4, :].rearrange("p t n -> p (t n)").bitcast(F32),
                                        ALU.subtract).then_inc(hidlo_b_made, 1)

            def step(s, tail=False, out=False, last=False):
                c = s - STEPS_IMG
                if out:
                    split_hidden(c - 1)
                if tail:
                    add_input_x(c)
                if not last:
                    split_lo(2 * s + 2, s + 1, 0)
                if tail:
                    split_cpin_x(c)
                    split_net(c, 0)
                if not last:
                    split_lo(2 * s + 3, s + 1, 1)

            pool.sem_inc(hidlo_b_made, 1)
            for b in range(T):
                split_lo(b, 0, b)
            scale_mlp()
            step(0)
            split_mlp()
            with pool.Fori(1, STEPS_IMG) as s:
                step(s)
            step(STEPS_IMG, tail=True)
            with pool.Fori(STEPS_IMG + 1, STEPS - 1) as s:
                step(s, tail=True, out=True)
            step(STEPS - 1, tail=True, out=True, last=True)

            def last_image(c, buf, more=True):
                if more:
                    add_input_x(c + 1, 1)
                    split_cpin_x(c + 1, 1)
                split_hidden(c)
                if more:
                    split_net(c + 1, 1 - buf)

            split_hidden(LAST - 1)
            add_input_x(LAST, 1)
            split_cpin_x(LAST, 1)
            split_net(LAST, 1)
            with pool.Fori(LAST, STEPS - 1, 2) as c:
                last_image(c, 1)
                last_image(c + 1, 0)
            last_image(STEPS - 1, 1, more=False)


def kernel(**inputs):
    import numpy as np
    import concourse.bacc as bacc
    from concourse.bass_utils import run_bass_kernel_spmd

    p = {k.removeprefix("L0_conv_"): np.asarray(v) for k, v in inputs.items()}

    def columns(v):
        return v.reshape(-1, P).T

    col = np.concatenate([columns(p[n]) for n in ("xq_b", "yq_b", "xv_b", "yv_b", "xp_b", "yp_b", "cp_b", "m1_b",
                                                  "m2_b", "ls1", "ls2")], axis=1)
    w = 2 * L - 1
    rel_rows = np.stack([p["rel_x"], p["rel_y"]])[:, :, :w][:, :, ::-1]
    arrays = {
        "x": p["x"].reshape(B, DIM, HW),
        "wq": np.stack([p["xq_w"], p["yq_w"]]),
        "wk": np.stack([p["xk_w"], p["yk_w"]]),
        "wv": np.stack([p["xv_w"], p["yv_w"]]),
        "wpT": np.stack([p["xp_w"].T, p["yp_w"].T]),
        "cpT": p["cp_w"].T,
        "m1T": p["m1_w"].T,
        "m2T": p["m2_w"].T,
        "columns": col,
        "ls_rows": np.stack([p["ls1"].reshape(-1), p["ls2"].reshape(-1)]),
        "rel_tiled": np.tile(rel_rows, (1, 1, L)),
    }
    arrays = {k: np.ascontiguousarray(v) for k, v in arrays.items()}
    nc = bacc.Bacc("TRN2", target_bir_lowering=False, num_devices=1)
    args = [nc.dram_tensor(k, v.shape, mybir.dt.from_np(v.dtype), kind="ExternalInput").ap() for k, v in arrays.items()]
    o = nc.dram_tensor("out", (B, DIM, HW), F32, kind="ExternalOutput").ap()
    axial_block_kernel(nc, *args, o)
    r = run_bass_kernel_spmd(nc, [arrays], core_ids=[0])
    return r.results[0]["out"].reshape(B, DIM, L, L)
```
